# Optimizing a Trainium2 kernel written in Bass

```python
import numpy as np
import jax
import jax.numpy as jnp

def _softmax(x, axis=-1):
    return jax.nn.softmax(x, axis=axis)

def _gelu(x):
    return jax.nn.gelu(x, approximate=True)

def _silu(x):
    return jax.nn.silu(x)

def _sigmoid(x):
    return jax.nn.sigmoid(x)

def _layernorm(x, axis=-1, eps=1e-05):
    m = jnp.mean(x, axis=axis, keepdims=True)
    v = jnp.var(x, axis=axis, keepdims=True)
    return (x - m) / jnp.sqrt(v + eps)

def _scatter_add(tgt, idx, src, axis=0):
    return tgt.at[idx].add(src)

def _segment_sum(src, seg, n):
    return jax.ops.segment_sum(src, seg, n)
kernel_name = 'mk_decoder_postln_d1_seqx_r8_9449c5'

def setup_inputs(seed: int=0):
    np.random.seed(seed)
    _w = jnp.asarray

    def _rec_inputs():
        import jax
        import jax.numpy as jnp
        _rk = jax.random.key(seed)
        x = 7.22e-05 + 1 * jax.random.normal(jax.random.fold_in(_rk, 1), (32, 64, 128), jnp.float32)
        _lenS = 64 - jax.random.randint(jax.random.fold_in(_rk, 7), (32,), 0, max(1, 64 // 4) + 1, jnp.int32)
        _lenS2 = 64 - jax.random.randint(jax.random.fold_in(_rk, 8), (32,), 0, max(1, 64 // 4) + 1, jnp.int32)
        _ctx_1024P = jax.random.normal(jax.random.fold_in(_rk, 11), (32, 16, 128), jnp.float32)
        _ctx_1024c = jax.random.dirichlet(jax.random.fold_in(_rk, 511), 0.3 * jnp.ones((16,), jnp.float32), (32, 64))
        _ctx_1024t = jnp.einsum('bsk,bkd->bsd', _ctx_1024c, _ctx_1024P)
        _ctx_1024t = _ctx_1024t * jax.lax.rsqrt(jnp.mean(jnp.square(_ctx_1024t)) + 1e-12) * 0.953939
        ctx_1024 = 4.13588e-05 + 0.999923 * (_ctx_1024t + 0.3 * jax.random.normal(jax.random.fold_in(_rk, 611), (32, 64, 128), jnp.float32))
        _validS = jnp.arange(64)[None, :] < _lenS[:, None]
        _validS2 = jnp.arange(64)[None, :] < _lenS2[:, None]
        _causal = jnp.tril(jnp.ones((64, 64), dtype=bool))
        mask_BxS2_bf1 = jnp.ones((32, 64), dtype=bool)
        return (x, ctx_1024, mask_BxS2_bf1)
    x, ctx_1024, mask_BxS2_bf1 = _rec_inputs()

    def _L0_attn_setup():
        import jax, jax.numpy as jnp
        import numpy as np
        import math
        D_MODEL = 128
        N_HEADS = 16
        D_HEAD = D_MODEL // N_HEADS
        SEQ = 256
        BATCH = 2
        key = jax.random.key(seed)
        ks = jax.random.split(key, 8)
        xav = math.sqrt(2.0 / (D_MODEL + D_MODEL))

        def lin(k):
            return jax.random.normal(k, (D_MODEL, D_MODEL), jnp.float32) * xav
        zeros = jnp.zeros((D_MODEL,), jnp.float32)
        return {'x': jax.random.normal(ks[0], (SEQ, BATCH, D_MODEL), jnp.float32), 'beta': jax.random.normal(ks[1], (N_HEADS,), jnp.float32) * 0.1, 'Wq': lin(ks[2]), 'bq': zeros, 'Wk': lin(ks[3]), 'bk': zeros, 'Wv': lin(ks[4]), 'bv': zeros, 'Wo': lin(ks[5]), 'bo': zeros}
    _L0_attn_all = _L0_attn_setup()
    _L0_attn_in = {k: v for k, v in _L0_attn_all.items() if k in ('beta', 'Wq', 'bq', 'Wk', 'bk', 'Wv', 'bv', 'Wo', 'bo')}
    del _L0_attn_all

    def _L0_xattn_setup():
        import jax, jax.numpy as jnp
        import numpy as np
        THETA = 10000.0

        def _rope_tables(T, head_dim, dtype):
            exps = jnp.arange(1, head_dim + 1, 2, dtype=jnp.float32)[:head_dim // 2] / head_dim
            w = 1.0 / THETA ** exps
            t = jnp.arange(1, T + 1, dtype=jnp.float32)
            angles = t[:, None] * w[None, :]
            return (jnp.sin(angles).astype(dtype), jnp.cos(angles).astype(dtype))

        def _rotate(x, sin, cos):
            x1 = x[..., ::2]
            x2 = x[..., 1::2]
            x1p = x1 * cos - x2 * sin
            x2p = x1 * sin + x2 * cos
            return jnp.stack((x1p, x2p), axis=-1).reshape(x.shape)
        key = jax.random.key(seed)
        B, Tq, Tkv, C = (4, 256, 256, 128)
        k1, k2, k3, k4, k5 = jax.random.split(key, 5)
        s = 1.0 / np.sqrt(C)
        return {'x_q': jax.random.normal(k1, (B, Tq, C), dtype=jnp.float32), 'x_kv': jax.random.normal(k2, (B, Tkv, C), dtype=jnp.float32), 'q_tok_mask': jnp.ones((B, Tq), dtype=bool), 'kv_tok_mask': jnp.ones((B, Tkv), dtype=bool), 'W_q': jax.random.normal(k3, (C, C), dtype=jnp.float32) * s, 'W_kv': jax.random.normal(k4, (C, 2 * C), dtype=jnp.float32) * s, 'W_c': jax.random.normal(k5, (C, C), dtype=jnp.float32) * s}
    _L0_xattn_all = _L0_xattn_setup()
    _L0_xattn_in = {k: v for k, v in _L0_xattn_all.items() if k in ('W_q', 'W_kv', 'W_c')}
    del _L0_xattn_all

    def _L0_ffn_setup():
        import jax, jax.numpy as jnp
        import numpy as np
        N_EMBD = 128
        N_EXP = 8
        TOP_K = 2
        CAPACITY = 512
        D_FF = 3 * N_EMBD
        key = jax.random.key(seed)
        k1, k2, k3, k4 = jax.random.split(key, 4)
        x = jax.random.normal(k1, (8, 256, N_EMBD), dtype=jnp.float32)
        w_gate = jax.random.normal(k2, (N_EMBD, N_EXP), dtype=jnp.float32) * 0.02
        c_fc = jax.random.normal(k3, (N_EXP, N_EMBD, D_FF), dtype=jnp.float32) * 0.02
        c_proj = jax.random.normal(k4, (N_EXP, D_FF // 2, N_EMBD), dtype=jnp.float32) * 0.02
        return {'x': x, 'w_gate': w_gate, 'c_fc': c_fc, 'c_proj': c_proj}
    _L0_ffn_all = _L0_ffn_setup()
    _L0_ffn_in = {k: v for k, v in _L0_ffn_all.items() if k in ('w_gate', 'c_fc', 'c_proj')}
    del _L0_ffn_all
    return {'x': x, 'ctx_1024': ctx_1024, 'mask_BxS2_bf1': mask_BxS2_bf1, 'L0_attn_beta': _L0_attn_in['beta'], 'L0_attn_Wq': _L0_attn_in['Wq'], 'L0_attn_bq': _L0_attn_in['bq'], 'L0_attn_Wk': _L0_attn_in['Wk'], 'L0_attn_bk': _L0_attn_in['bk'], 'L0_attn_Wv': _L0_attn_in['Wv'], 'L0_attn_bv': _L0_attn_in['bv'], 'L0_attn_Wo': _L0_attn_in['Wo'], 'L0_attn_bo': _L0_attn_in['bo'], 'L0_xattn_W_q': _L0_xattn_in['W_q'], 'L0_xattn_W_kv': _L0_xattn_in['W_kv'], 'L0_xattn_W_c': _L0_xattn_in['W_c'], 'L0_ffn_w_gate': _L0_ffn_in['w_gate'], 'L0_ffn_c_fc': _L0_ffn_in['c_fc'], 'L0_ffn_c_proj': _L0_ffn_in['c_proj']}

def reference(x, ctx_1024, mask_BxS2_bf1, L0_attn_beta, L0_attn_Wq, L0_attn_bq, L0_attn_Wk, L0_attn_bk, L0_attn_Wv, L0_attn_bv, L0_attn_Wo, L0_attn_bo, L0_xattn_W_q, L0_xattn_W_kv, L0_xattn_W_c, L0_ffn_w_gate, L0_ffn_c_fc, L0_ffn_c_proj):
    import jax
    import jax.numpy as jnp

    def _L0_attn_ref(x, beta, Wq, bq, Wk, bk, Wv, bv, Wo, bo):
        import jax, jax.numpy as jnp
        import numpy as np
        import math
        D_MODEL = 128
        N_HEADS = 16
        D_HEAD = D_MODEL // N_HEADS
        SEQ = 256
        BATCH = 2
        s, b, d = x.shape
        h, dh = (N_HEADS, D_HEAD)

        def proj(W, bias):
            y = x @ W.T + bias
            return y.reshape(s, b, h, dh).transpose(1, 2, 0, 3)
        q = proj(Wq, bq)
        k = proj(Wk, bk)
        v = proj(Wv, bv)
        scale = math.sqrt(dh) * jnp.exp(beta)[None, :, None, None]
        q = jax.nn.softplus(q / scale)
        k = jax.nn.softplus(k / scale)
        kv = jnp.cumsum(k[..., :, None] * v[..., None, :], axis=2)
        kn = jnp.cumsum(k, axis=2)
        num = jnp.einsum('bhsk,bhskv->bhsv', q, kv)
        den = jnp.einsum('bhsk,bhsk->bhs', q, kn)
        out = num / den[..., None]
        out = out.transpose(2, 0, 1, 3).reshape(s, b, d)
        return out @ Wo.T + bo

    def _L0_xattn_ref(x_q, x_kv, q_tok_mask, kv_tok_mask, W_q, W_kv, W_c):
        import jax, jax.numpy as jnp
        import numpy as np
        THETA = 10000.0

        def _rope_tables(T, head_dim, dtype):
            exps = jnp.arange(1, head_dim + 1, 2, dtype=jnp.float32)[:head_dim // 2] / head_dim
            w = 1.0 / THETA ** exps
            t = jnp.arange(1, T + 1, dtype=jnp.float32)
            angles = t[:, None] * w[None, :]
            return (jnp.sin(angles).astype(dtype), jnp.cos(angles).astype(dtype))

        def _rotate(x, sin, cos):
            x1 = x[..., ::2]
            x2 = x[..., 1::2]
            x1p = x1 * cos - x2 * sin
            x2p = x1 * sin + x2 * cos
            return jnp.stack((x1p, x2p), axis=-1).reshape(x.shape)
        B, Tq, C = x_q.shape
        Tkv = x_kv.shape[1]
        H = 16
        D = C // H
        q = (x_q @ W_q).reshape(B, Tq, H, D).transpose(0, 2, 1, 3)
        kv = x_kv @ W_kv
        k, v = (kv[..., :C], kv[..., C:])
        k = k.reshape(B, Tkv, H, D).transpose(0, 2, 1, 3)
        v = v.reshape(B, Tkv, H, D).transpose(0, 2, 1, 3)
        sin_q, cos_q = _rope_tables(Tq, D, x_q.dtype)
        sin_k, cos_k = _rope_tables(Tkv, D, x_q.dtype)
        q = _rotate(q, sin_q, cos_q)
        k = _rotate(k, sin_k, cos_k)
        att = jnp.einsum('bhqd,bhkd->bhqk', q, k) / jnp.sqrt(jnp.asarray(D, x_q.dtype))
        mask = (q_tok_mask[:, :, None] & kv_tok_mask[:, None, :])[:, None, :, :]
        att = jnp.where(mask, att, jnp.asarray(-1000000000.0, att.dtype))
        att = jax.nn.softmax(att, axis=-1)
        y = jnp.einsum('bhqk,bhkd->bhqd', att, v)
        y = y.transpose(0, 2, 1, 3).reshape(B, Tq, C)
        return y @ W_c

    def _L0_ffn_ref(x, w_gate, c_fc, c_proj):
        import jax, jax.numpy as jnp
        import numpy as np
        N_EMBD = 128
        N_EXP = 8
        TOP_K = 2
        CAPACITY = 512
        D_FF = 3 * N_EMBD
        B, T, d = x.shape
        N = B * T
        xf = x.reshape(N, d)
        scores = jax.nn.softmax(xf @ w_gate, axis=-1)
        weights, idx = jax.lax.top_k(scores, TOP_K)
        flat_e = idx.reshape(-1)
        tok = jnp.repeat(jnp.arange(N), TOP_K)
        oh = jax.nn.one_hot(flat_e, N_EXP, dtype=jnp.int32)
        pos = (jnp.cumsum(oh, axis=0) * oh).sum(-1) - 1
        valid = pos < CAPACITY
        pos_c = jnp.where(valid, pos, 0)
        vmask = valid.astype(x.dtype)[:, None]
        exp_x = jnp.zeros((N_EXP, CAPACITY, d), x.dtype)
        exp_x = exp_x.at[flat_e, pos_c].add(xf[tok] * vmask)
        h = jnp.einsum('ecd,edf->ecf', exp_x, c_fc)
        a, g = jnp.split(h, 2, axis=-1)
        h = jax.nn.silu(a) * g
        exp_out = jnp.einsum('ecf,efd->ecd', h, c_proj)
        gathered = exp_out[flat_e, pos_c]
        w = weights.reshape(-1)[:, None] * vmask
        out = (gathered * w).reshape(N, TOP_K, d).sum(axis=1)
        return out.reshape(B, T, d)
    x = _layernorm(x + _L0_attn_ref(x, L0_attn_beta, L0_attn_Wq, L0_attn_bq, L0_attn_Wk, L0_attn_bk, L0_attn_Wv, L0_attn_bv, L0_attn_Wo, L0_attn_bo), axis=-1)
    x = _layernorm(x + _L0_xattn_ref(x, ctx_1024, mask_BxS2_bf1, mask_BxS2_bf1, L0_xattn_W_q, L0_xattn_W_kv, L0_xattn_W_c), axis=-1)
    x = _layernorm(x + _L0_ffn_ref(x, L0_ffn_w_gate, L0_ffn_c_fc, L0_ffn_c_proj), axis=-1)
    return x

_drawn_inputs = setup_inputs


def setup_inputs(seed=0):
    import zlib

    import numpy as np

    out = dict(_drawn_inputs(seed))
    spreads = {'L0_attn_bq': (0.0, 0.8),
     'L0_attn_bk': (0.0, 0.8),
     'L0_attn_bv': (0.0, 0.1),
     'L0_attn_bo': (0.0, 0.1)}
    factors = {'L0_attn_beta': 8.0,
     'L0_attn_Wq': 8.0,
     'L0_ffn_w_gate': 8.0,
     'L0_ffn_c_fc': 8.0,
     'L0_ffn_c_proj': 8.0}
    for name, (base, spread) in spreads.items():
        noise = np.random.default_rng([zlib.crc32(name.encode()), seed]).standard_normal(out[name].shape)
        drawn = base * np.exp(spread * noise) if base else spread * noise
        out[name] = jnp.asarray(drawn.astype(out[name].dtype))
    for name, factor in factors.items():
        out[name] = (out[name] * factor).astype(out[name].dtype)
    return out
```

```python
from contextlib import ExitStack

import numpy as np

import concourse.bass as bass
from concourse import mybir

ALU = mybir.AluOpType
ACT = mybir.ActivationFunctionType
AX = mybir.AxisListType
F32 = mybir.dt.float32
BF16 = mybir.dt.bfloat16
U32 = mybir.dt.uint32
U8 = mybir.dt.uint8

S, B, C = 32, 64, 128
N = S * B
H, D = 16, 8
T = 128
NT = N // T
CT = 4
CH = CT * T
NC = N // CH
G = 4
I = H // G
V9 = D + 1
E, K2, CAP = 8, 2, 512
F = 192
FR = F - 128
ROW = C + 2
RB = 8
EPS = 1e-5
UNUSED = 1e6

K_ID, K_TRI, K_CAUSAL = 0, 128, 256
K_COSQ, K_SINQ, K_COSK, K_SINK = 288, 352, 416, 480
K_RANK, K_BASE, K_COEF = 544, 552, 560
K_COLS = 576


def constants():
    k = np.zeros((128, K_COLS), np.float32)
    k[:, K_ID:K_ID + 128] = np.eye(128)
    k[:, K_TRI:K_TRI + 128] = np.triu(np.ones((128, 128)), 1)
    s = np.arange(S)
    k[:, K_CAUSAL:K_CAUSAL + S] = (s[None, :] >= (np.arange(128) % S)[:, None])
    w = (1.0 / np.float32(10000.0) ** (np.arange(1, D + 1, 2, dtype=np.float32) / np.float32(D))).astype(np.float32)
    angle = np.arange(1, B + 1, dtype=np.float32)[None, :] * w[(np.arange(C) % D) // 2][:, None]
    sign = np.where(np.arange(C) % 2 == 0, -1.0, 1.0)[:, None]
    scale = 1.0 / np.sqrt(np.float64(D))
    k[:, K_COSQ:K_COSQ + B] = np.cos(angle) * scale
    k[:, K_SINQ:K_SINQ + B] = np.sin(angle) * sign * scale
    k[:, K_COSK:K_COSK + B] = np.cos(angle)
    k[:, K_SINK:K_SINK + B] = np.sin(angle) * sign
    k[:, K_RANK:K_RANK + E] = E - np.arange(E)
    k[:, K_BASE:K_BASE + E] = CAP * np.arange(E)
    rest = np.float64(-1e9)
    for r in range(3):
        bits = np.array([rest], np.float32).view(np.uint32) & np.uint32(0xFFFF0000)
        part = bits.view(np.float32)[0]
        k[r, K_COEF:K_COEF + 3] = (1.0, part, -part)
        rest -= np.float64(part)
    assert rest == 0
    k[:, K_COEF + 3] = EPS
    dest = (np.arange(NT)[None, :, None] * T + np.arange(T)[:, None, None] + N * np.arange(K2)[None, None, :])
    blank = np.zeros((128, 4, ROW), np.float32)
    blank.view(np.uint32)[:, :, C] = int(UNUSED)
    return k, dest.astype(np.uint32).reshape(128, NT * K2), blank.reshape(128, 4 * ROW)


def decoder_layer(nc, xT_d, ctxT_d, mask_d, cols_d, bv_d, w1_d, w2_d, wg_d, fc_d, proj_d, const_d, dest_d, blank_d, out):
    with ExitStack() as ctx:
        def sb(name, shape, dt=F32):
            return ctx.enter_context(nc.sbuf_tensor(name, shape, dt))

        def sem(name):
            return ctx.enter_context(nc.semaphore(name))

        slots_d = nc.dram_tensor("slots_d", (E * CAP, ROW), F32, kind="Internal").ap()
        picks_d = nc.dram_tensor("picks_d", (K2 * N, C), F32, kind="Internal").ap()

        xT = sb("xT", [128, N])
        ctxT = sb("ctxT", [128, N])
        x1T = sb("x1T", [128, N])
        w1 = sb("w1", [128, 4, 128])
        w2 = sb("w2", [128, 6, 128])
        wg = sb("wg", [128, E])
        fc = sb("fc", [128, E, 2 * F])
        pj0 = sb("pj0", [128, E, C])
        pj1 = sb("pj1", [128, E, C])
        cst = sb("cst", [128, K_COLS])
        cols = sb("cols", [128, 4])
        scol = sb("scol", [128, 4])
        bvb = sb("bvb", [128, C])
        dest = sb("dest", [128, NT, K2], U32)
        tri = sb("tri", [128, 128], BF16)
        ones = sb("ones", [128, 128], BF16)
        mask8 = sb("mask8", [128, N], U8)
        cosq = sb("cosq", [128, N])
        sinq = sb("sinq", [128, N])
        mrow = sb("mrow", [128, N], BF16)
        nrow = sb("nrow", [128, N], BF16)
        wide = [sb(f"wide{i}", [128, H, CH]) for i in range(2)]
        soft = sb("soft", [128, 8, CH])
        work = sb("work", [128, 4, CH])
        early = sb("early", [128, N + 2 * CH + 2 * H * G * V9])
        Vb2 = [sb(f"Vb2_{i}", [128, 2, H, G, V9]) for i in range(2)]
        x1pair = sb("x1pair", [128, 2, CT, C])
        x1n = [x1pair[:, i, :, :] for i in range(2)]
        blank_sb = x1pair[:, :, :, :].rearrange("p a t c -> p (a t c)")[:, 0:4 * ROW]
        x2T = sb("x2T", [128, CH])
        rden = sb("rden", [128, 2, I, G])
        O = [sb(f"O{i}", [128, G, I, D]) for i in range(2)]
        OT = [sb(f"OT{i}", [128, T]) for i in range(2 * CT)]
        stats = sb("stats", [128, 3 * NT, 6])
        mv = sb("mv", [128, 3 * NT, 2])
        lnv = sb("lnv", [128, 3 * NT])
        r0 = sb("r0", [128, 3 * NT])
        r1 = sb("r1", [128, 3 * NT])
        rstd = sb("rstd", [128, 3 * NT])
        mx2 = sb("mx2", [128, 2, H])
        xlin, ebuf, lbuf, wbuf = ([soft[:, 2 * n + i, :] for i in range(2)] for n in range(4))
        qT, kT = ([work[:, 2 * n + i, :] for i in range(2)] for n in range(2))
        xb = early[:, 0:N]
        P1 = [early[:, N + i * CH:N + (i + 1) * CH].rearrange("p (h s) -> p h s", s=S) for i in range(2)]
        Vb1 = [early[:, N + 2 * CH + i * H * G * V9:N + 2 * CH + (i + 1) * H * G * V9]
               .rearrange("p (h g v) -> p h g v", h=H, g=G) for i in range(2)]
        xrow = early[:, 0:NT * K2 * ROW].rearrange("p (t k n) -> p t k n", t=NT, k=K2)
        maskf = x1T
        qT2, kT2 = ([xT[:, (2 * n + i) * CH:(2 * n + i + 1) * CH] for i in range(2)] for n in range(2))
        ra, rb = xlin, ebuf
        SC = [soft[:, 4 + 2 * i:6 + 2 * i, :].rearrange("p a (h b) -> p (a h) b", b=B) for i in range(2)]
        PT = [work[:, 2 * i:2 * i + 2, :].rearrange("p a (h k s) -> p (a h) k s", k=2, s=S) for i in range(2)]
        et = [x1T[:, i * CT * ROW:(i + 1) * CT * ROW].rearrange("p (j n) -> p j n", j=CT) for i in range(2)]
        xeT = xlin
        sil = [soft[:, 4 + 2 * i:6 + 2 * i, :] for i in range(2)]
        hid = [work[:, 2 * i:2 * i + 2, :] for i in range(2)]
        ys = x1n
        gl = sb("gl", [128, CT, E])
        ge = sb("ge", [128, CT, E])
        gs = sb("gs", [128, CT, E])
        g1 = sb("g1", [128, CT])
        gm = sb("gm", [128, K2, CT])
        gt = sb("gt", [128, CT, E])
        pick = sb("pick", [128, K2, CT, E])
        mem = sb("mem", [128, CT + 1, E], BF16)
        carry = [sb(f"carry{i}", [128, E]) for i in range(2)]
        pos = sb("pos", [128, CT, E])
        pp = sb("pp", [128, K2, CT, E])
        pq = sb("pq", [128, K2, CT, E])
        psel = sb("psel", [128, K2, CT])
        bsel = sb("bsel", [128, K2, CT])
        over = sb("over", [128, K2, CT])
        slot = sb("slot", [128, NT, K2], U32)
        Y = [wide[i][:, 0:4, :].rearrange("p a (t c) -> p (a t) c", c=C) for i in range(2)]
        Z = wide[0][:, 4:8, :].rearrange("p a (t c) -> p (a t) c", c=C)
        R = wide[1][:, 4:8, :].rearrange("p a (t c) -> p (a t) c", c=C)

        PS = [ctx.enter_context(nc.psum_tensor(f"PS{i}", [128, 512], F32)) for i in range(3)]
        PSS = [ctx.enter_context(nc.psum_tensor(f"PSS{i}", [128, 2, 512], F32)) for i in range(2)]
        PS7 = ctx.enter_context(nc.psum_tensor("PS7", [128, 512], F32))

        ld_x = [sem(f"ld_x{c}") for c in range(NC)]
        ld_w1, ld_cst, ld_cols, ld_bv = sem("ld_w1"), sem("ld_cst"), sem("ld_cols"), sem("ld_bv")
        ld_ctx, ld_w2, ld_mask, ld_dest = sem("ld_ctx"), sem("ld_w2"), sem("ld_mask"), sem("ld_dest")
        ld_wg, ld_fc, ld_pj, ld_blank = sem("ld_wg"), sem("ld_fc"), sem("ld_pj"), sem("ld_blank")
        z_wide = [sem(f"z_wide{i}") for i in range(2)]
        z_small, z_vb = sem("z_small"), sem("z_vb")
        init_d = sem("init_d")
        widened = [sem(f"widened{i}") for i in range(2)]
        act_chain, dve_chain, pool_chain = sem("act_chain"), sem("dve_chain"), sem("pool_chain")
        sc_ready, xb_ready = sem("sc_ready"), sem("xb_ready")
        tabs_ready, rows_ready, ones_ready = sem("tabs_ready"), sem("rows_ready"), sem("ones_ready")
        pe_qk, pe_v1, pe_s1, pe_pv, pe_out, pe_t1 = (sem(n) for n in ("pe_qk", "pe_v1", "pe_s1", "pe_pv", "pe_out", "pe_t1"))
        sp_abs, sp_lin, sp_exp, sp_ln, sp_done = (sem(n) for n in ("sp_abs", "sp_lin", "sp_exp", "sp_ln", "sp_done"))
        p1_ready, v1_ready = sem("p1_ready"), sem("v1_ready")
        o_norm, o_ready = sem("o_norm"), sem("o_ready")
        mv_ready, r0_ready, normed = sem("mv_ready"), sem("r0_ready"), sem("normed")
        x1T_ready = sem("x1T_ready")
        pe_rope, rope_mul, rope_done = sem("pe_rope"), sem("rope_mul"), sem("rope_done")
        pe_v2, v2_ready, pe_s2, sub_done, exp_done, pt_ready = (
            sem(n) for n in ("pe_v2", "v2_ready", "pe_s2", "sub_done", "exp_done", "pt_ready"))
        pe_t2, x2T_ready, pe_gate, gate_sub, gate_exp, mem_ready, pe_cum, slot_ready = (
            sem(n) for n in ("pe_t2", "x2T_ready", "pe_gate", "gate_sub", "gate_exp", "mem_ready", "pe_cum", "slot_ready"))
        scattered = sem("scattered")
        et_in = [sem(f"et_in{i}") for i in range(2)]
        pe_te, xeT_ready, pe_h, sil_ready, hid_ready, pe_y, ys_ready = (
            sem(n) for n in ("pe_te", "xeT_ready", "pe_h", "sil_ready", "hid_ready", "pe_y", "ys_ready"))
        picked = [sem(f"picked{i}") for i in range(2)]
        y_in = [sem(f"y_in{c}") for c in range(NC)]
        y_sum, stored = sem("y_sum"), sem("stored")

        def col(a, b=None):
            return cst[:, a:(a + 1 if b is None else b)]

        ident = cst[:, K_ID:K_ID + 128]
        ROPES = [(w, c) for c in range(NC) for w in "kq"]

        def out_psum(t):
            return (PSS[1][:, 0, :] if t < NT else PS[0])[:, (t % CT) * 128:(t % CT) * 128 + 128]

        pv_psum = PS7[:, 0:I * G * V9]
        gate_psum = PS[0][:, 0:CT * E]
        cum_psum = PS[1][:, 0:(CT + 1) * E]

        def scatter(pool, c):
            if c == 0:
                pool.wait_ge(init_d, 16 * 2 * E)
            pool.wait_ge(slot_ready, c + 1)
            for t in range(c * CT, (c + 1) * CT):
                for k in range(K2):
                    pool.indirect_dma_start(out=slots_d, out_offset=bass.IndirectOffsetOnAxis(ap=slot[:, t, k:k + 1], axis=0),
                                            in_=xrow[:, t, k, :], in_offset=None,
                                            bounds_check=E * CAP - 1, oob_is_err=False).then_inc(scattered, 16)

        def weigh(act, e):
            act.wait_ge(pe_y, e + 1)
            if e >= 2:
                act.wait_ge(picked[e % 2], 16 * CT * (e // 2))
            for j in range(CT):
                act.activation(ys[e % 2][:, j, :], PS7[:, j * C:(j + 1) * C], ACT.Copy,
                               scale=et[e % 2][:, j, C + 1:C + 2]).then_inc(ys_ready, 1)

        def expert_psum(e):
            if e % 2:
                return PSS[1][:, 0, :], PSS[1][:, 1, :], PS[1][:, :]
            return PSS[0][:, 0, :], PSS[0][:, 1, :], PS[2][:, :]

        def rope_products(dve, n):
            w, c = ROPES[n]
            dve.wait_ge(pe_rope, n + 1)
            if n == 1:
                dve.wait_ge(tabs_ready, 2)
            if n >= 2:
                dve.wait_ge(rope_done, n - 1)
            if w == "k":
                cos = cst[:, None, K_COSK:K_COSK + B].to_broadcast([128, CH // B, B])
                sin = cst[:, None, K_SINK:K_SINK + B].to_broadcast([128, CH // B, B])
            else:
                cos, sin = (tab[:, c * CH:(c + 1) * CH].rearrange("p (s b) -> p s b", b=B) for tab in (cosq, sinq))
            v = lambda ap: ap[:, :].rearrange("p (s b) -> p s b", b=B)
            dve.tensor_tensor(v(ra[n % 2]), v(PS[0]), cos, ALU.mult)
            dve.tensor_tensor(v(rb[n % 2]), v(PS[1]), sin, ALU.mult).then_inc(rope_mul, 1)

        block = ctx.enter_context(nc.Block())

        @block.sync
        def _(sp):
            sp.dma_start(w1[:, :, :], w1_d.rearrange("p (a n) -> p a n", a=4)).then_inc(ld_w1, 16)
            for c in range(NC):
                sp.dma_start(xT[:, c * CH:(c + 1) * CH], xT_d[:, c * CH:(c + 1) * CH]).then_inc(ld_x[c], 16)
            sp.dma_start(ctxT[:, :], ctxT_d).then_inc(ld_ctx, 16)
            sp.dma_start(w2[:, :, :], w2_d.rearrange("p (a n) -> p a n", a=6)).then_inc(ld_w2, 16)

            def widen(u, src, done, n):
                sp.wait_ge(done, n)
                if u < 2:
                    sp.wait_ge(z_wide[u], 1)
                    if u == 1:
                        sp.wait_ge(init_d, 16 * 2 * E)
                elif u - 2 < NC:
                    sp.wait_ge(pe_s1, CT * (u - 1))
                else:
                    sp.wait_ge(pe_s2, CT * (u - 1 - NC))
                for h in range(H):
                    sp.dma_start(wide[u % 2][D * h:D * h + D, h, :], src[D * h:D * h + D, :]).then_inc(widened[u % 2], 16)

            for c in range(NC):
                widen(c, qT[c % 2], sp_done, 2 * c + 1)
                if c == 0:
                    sp.dma_start(fc[:, :, :], fc_d.rearrange("p (e f) -> p e f", e=E)).then_inc(ld_fc, 16)
                    sp.dma_start(pj0[:, :, :], proj_d[:, 0:128, :].rearrange("e p n -> p e n")).then_inc(ld_pj, 16)
                    sp.wait_ge(z_small, 1)
                    sp.dma_start(pj1[64:128, :, :], proj_d[:, 128:F, :].rearrange("e p n -> p e n")).then_inc(ld_pj, 16)
                    sp.dma_start(wg[:, :], wg_d).then_inc(ld_wg, 16)
                    sp.wait_ge(ld_blank, 16)
                    sp.wait_ge(z_wide[1], 1)
                    for e in range(E):
                        sp.dma_start(slots_d[e * CAP:(e + 1) * CAP, :].rearrange("(p j) n -> p (j n)", j=4), blank_sb[:, :]).then_inc(init_d, 16)
                        sp.dma_start(picks_d[e * CAP:(e + 1) * CAP, :].rearrange("(p j) n -> p (j n)", j=4), wide[1][:, H - 1, :]).then_inc(init_d, 16)
            for c in range(NC):
                widen(NC + c, kT2[c % 2], rope_done, ROPES.index(("k", c)) + 1)
            sp.wait_ge(scattered, 16 * NT * K2)
            for e in range(E):
                if e >= 2:
                    sp.wait_ge(picked[e % 2], 16 * CT * (e // 2))
                sp.dma_start(et[e % 2][:, :, :], slots_d[e * CAP:(e + 1) * CAP, :].rearrange("(p j) n -> p j n", j=CT)).then_inc(et_in[e % 2], 16)
            for i in range(2):
                sp.wait_ge(picked[i], 16 * CT * (E // 2))
            for c in range(NC):
                for k in range(K2):
                    sp.dma_start(Y[k][:, c * CT:(c + 1) * CT, :],
                                 picks_d[k * N + c * CH:k * N + (c + 1) * CH, :].rearrange("(t p) n -> p t n", p=T)).then_inc(y_in[c], 16)
            out_v = out.rearrange("s b n -> (s b) n").rearrange("(t p) n -> p t n", p=T)
            for c in range(NC):
                sp.wait_ge(normed, 2 * NT + CT * (c + 1))
                sp.dma_start(out_v[:, c * CT:(c + 1) * CT, :], R[:, c * CT:(c + 1) * CT, :]).then_inc(stored, 16)
            sp.wait_ge(stored, 16 * NC)

        @block.gpsimd
        def _(pool):
            chain = [0]

            def link(ins):
                chain[0] += 1
                ins.then_inc(pool_chain, 1)
                pool.wait_ge(pool_chain, chain[0])

            pool.memset(pj1[:, :, :], 0.0).then_inc(z_small, 1)
            pool.memset(wide[1][:, :, :], 0.0).then_inc(z_wide[1], 1)
            pool.wait_ge(ld_cols, 16)
            for c in range(NC):
                pool.wait_ge(ld_x[c], 16)
            pool.tensor_scalar(xb[:, :], xT[:, :], cols[:, 3:4], None, ALU.add).then_inc(xb_ready, 1)
            pool.wait_ge(ld_mask, 16)
            pool.wait_ge(ld_cst, 16)
            link(pool.tensor_copy(maskf[:, :], mask8[:, :]))
            m3 = maskf[:, :].rearrange("p (s b) -> p s b", b=B)
            for tab, k in ((cosq, K_COSQ), (sinq, K_SINQ)):
                pool.tensor_tensor(tab[:, :].rearrange("p (s b) -> p s b", b=B), m3,
                                   cst[:, None, k:k + B].to_broadcast([128, S, B]), ALU.mult).then_inc(tabs_ready, 1)
            pool.tensor_scalar(mrow[:, :], maskf[:, :], col(K_COEF), None, ALU.mult).then_inc(rows_ready, 1)
            pool.tensor_scalar(nrow[:, :], maskf[:, :], col(K_COEF + 2), col(K_COEF + 1), ALU.mult, ALU.add).then_inc(rows_ready, 1)
            for n, (w, c) in enumerate(ROPES):
                pool.wait_ge(rope_mul, n + 1)
                if c >= 2 and w == "k":
                    pool.wait_ge(widened[c % 2], 16 * H * ((NC + c - 2) // 2 + 1))
                if c >= 2 and w == "q":
                    pool.wait_ge(pe_s2, CT * (c - 1))
                dst = kT2[c % 2] if w == "k" else qT2[c % 2]
                pool.tensor_tensor(dst[:, :], ra[n % 2][:, :], rb[n % 2][:, :], ALU.add).then_inc(rope_done, 1)
            for c in range(NC):
                scatter(pool, c)
            for e in range(E):
                for j in range(CT):
                    pool.wait_ge(ys_ready, CT * e + j + 1)
                    pool.indirect_dma_start(out=picks_d, out_offset=bass.IndirectOffsetOnAxis(ap=et[e % 2][:, j, C:C + 1].bitcast(U32), axis=0),
                                            in_=ys[e % 2][:, j, :], in_offset=None,
                                            bounds_check=K2 * N - 1, oob_is_err=False).then_inc(picked[e % 2], 16)
            for c in range(NC):
                pool.wait_ge(y_in[c], 32)
                pool.tensor_tensor(Z[:, c * CT:(c + 1) * CT, :], Y[0][:, c * CT:(c + 1) * CT, :], Y[1][:, c * CT:(c + 1) * CT, :], ALU.add).then_inc(y_sum, 1)

        @block.scalar
        def _(act):
            chain = [0]

            def link(ins):
                chain[0] += 1
                ins.then_inc(act_chain, 1)
                act.wait_ge(act_chain, chain[0])

            act.dma_start(cols[:, :], cols_d).then_inc(ld_cols, 16)
            act.dma_start(cst[:, :], const_d).then_inc(ld_cst, 16)
            act.dma_start(bvb[:, :], bv_d.to_broadcast([128, C])).then_inc(ld_bv, 16)
            act.dma_start(mask8[:, :], mask_d.to_broadcast([128, N])).then_inc(ld_mask, 16)
            act.dma_start(blank_sb[:, :], blank_d).then_inc(ld_blank, 16)
            act.dma_start(dest[:, :, :], dest_d.rearrange("p (t k) -> p t k", k=K2)).then_inc(ld_dest, 16)
            act.preload_act_table_set("natural_log_exp_and_others")
            act.wait_ge(ld_cols, 16)
            link(act.activation(scol[:, 3:4], cols[:, 0:1], ACT.Exp, scale=-1.0))
            link(act.mul(scol[:, 0:1], scol[:, 3:4], float(D) ** -0.5))
            for r in range(2):
                act.activation(scol[:, 1 + r:2 + r], cols[:, 1 + r:2 + r], ACT.Copy, scale=scol[:, 0:1]).then_inc(sc_ready, 1)
            act.wait_ge(sc_ready, 2)

            def softplus(c):
                for r in range(2):
                    n = 2 * c + r
                    act.wait_ge(pe_qk, n + 1)
                    if c:
                        act.wait_ge(sp_done, n - 1)
                    act.activation(ebuf[r][:, :], PS[r][:, :], ACT.Abs, scale=scol[:, 0:1], bias=scol[:, 1 + r:2 + r]).then_inc(sp_abs, 1)
                    act.activation(xlin[r][:, :], PS[r][:, :], ACT.Identity, scale=scol[:, 0:1], bias=scol[:, 1 + r:2 + r]).then_inc(sp_lin, 1)
                for r in range(2):
                    act.wait_ge(sp_abs, 2 * c + r + 1)
                    act.activation(ebuf[r][:, :], ebuf[r][:, :], ACT.Exp, scale=-1.0).then_inc(sp_exp, 1)
                for r in range(2):
                    act.wait_ge(sp_exp, 2 * c + r + 1)
                    act.activation(lbuf[r][:, :], ebuf[r][:, :], ACT.Ln, bias=1.0).then_inc(sp_ln, 1)

            def norm_start(c):
                a, b = c * CT, (c + 1) * CT
                act.wait_ge(mv_ready, b)
                act.wait_ge(ld_cst, 16)
                link(act.activation(lnv[:, a:b], mv[:, a:b, 1], ACT.Ln, bias=col(K_COEF + 3)))
                act.activation(r0[:, a:b], lnv[:, a:b], ACT.Exp, scale=-0.5).then_inc(r0_ready, 1)

            def x1T_copy(c):
                if c == 0:
                    act.wait_ge(rows_ready, 2)
                act.wait_ge(pe_t1, CT * (c + 1))
                dst = x1T[:, :].rearrange("p (s b) -> p b s", b=B)[:, c * 4 * CT:(c + 1) * 4 * CT, :]
                act.copy(dst, PSS[1][:, 1, :].rearrange("p (b s) -> p b s", s=S)).then_inc(x1T_ready, 1)

            for k in range(-CT, NT + 7):
                if k % CT == 0 and k // CT + 1 < NC:
                    softplus(k // CT + 1)
                if k >= 5 and (k - 5) % CT == 0 and (k - 5) // CT < NC:
                    norm_start((k - 5) // CT)
                if k >= 7 and (k - 7) % CT == 0 and (k - 7) // CT < NC:
                    x1T_copy((k - 7) // CT)

            def v2_copy(t):
                act.wait_ge(pe_v2, t + 1)
                if t == 0:
                    act.wait_ge(z_vb, 2)
                if t >= 2:
                    act.wait_ge(pe_pv, NT + t - 1)
                for g in range(G):
                    ps = slice(32 * g, 32 * g + 32)
                    ins = act.copy(Vb2[t % 2][ps, :, :, g, 0:D],
                                   PS[2][ps, 0:2 * C].rearrange("p (k h d) -> p k h d", k=2, h=H))
                ins.then_inc(v2_ready, 1)

            def exp2(t):
                act.wait_ge(sub_done, t + 1)
                act.activation(SC[t % 2][:, :, :], SC[t % 2][:, :, :], ACT.Exp).then_inc(exp_done, 1)

            def x2T_copy(c):
                act.wait_ge(pe_t2, c + 1)
                if c:
                    act.wait_ge(pe_gate, c)
                act.copy(x2T[:, :], PS[1][:, :]).then_inc(x2T_ready, 1)

            def gate_exp_step(c):
                act.wait_ge(gate_sub, c + 1)
                act.activation(ge[:, :, :], gl[:, :, :], ACT.Exp).then_inc(gate_exp, 1)

            for k in range(NT + 11):
                if k < NT:
                    v2_copy(k)
                    exp2(k)
                for off, step in ((7, lambda c: norm_start(NC + c)), (9, x2T_copy), (10, gate_exp_step)):
                    if k >= off and (k - off) % CT == 0 and (k - off) // CT < NC:
                        step((k - off) // CT)

            for e in range(E):
                act.wait_ge(pe_te, e + 1)
                if e >= 2:
                    act.wait_ge(pe_h, e - 1)
                act.copy(xeT[e % 2][:, :], PS[0][:, :]).then_inc(xeT_ready, 1)
                act.wait_ge(pe_h, e + 1)
                if e >= 2:
                    act.wait_ge(hid_ready, e - 1)
                pa, pm = expert_psum(e)[0], expert_psum(e)[2]
                act.activation(sil[e % 2][:, 0, :], pa, ACT.Silu)
                act.activation(sil[e % 2][64:128, 1, :], pm[0:64, :], ACT.Silu).then_inc(sil_ready, 1)
                if e:
                    weigh(act, e - 1)
            weigh(act, E - 1)
            act.preload_act_table_set("natural_log_exp_and_others")
            for c in range(NC):
                norm_start(2 * NC + c)

        @block.tensor
        def _(pe):
            def project1(c):
                pe.wait_ge(ld_x[c], 16)
                if c == 0:
                    pe.wait_ge(ld_w1, 16)
                for r in range(2):
                    if c:
                        pe.wait_ge(sp_lin, 2 * c - 1 + r)
                    pe.matmul(PS[r][:, :], w1[:, r, :], xT[:, c * CH:(c + 1) * CH], start=True, stop=True).then_inc(pe_qk, 1)

            def project_v1(c):
                if c:
                    pe.wait_ge(v1_ready, CT * c)
                for i in range(CT):
                    t = c * CT + i
                    ins = pe.matmul(PS[2][:, i * C:(i + 1) * C], xT[:, t * T:(t + 1) * T], w1[:, 2, :], start=True, stop=True)
                ins.then_inc(pe_v1, 1)

            def scores1(t):
                c, i = divmod(t, CT)
                if i == 0:
                    pe.wait_ge(sp_done, 2 * c + 2)
                    pe.wait_ge(widened[c % 2], 16 * H * (c // 2 + 1))
                if t >= 2:
                    pe.wait_ge(p1_ready, t - 1)
                for j in range(G):
                    a = i * T + j * S
                    ins = pe.matmul(PSS[0][32 * j:32 * j + 32, t % 2, :], kT[c % 2][:, a:a + S], wide[c % 2][:, :, a:a + S],
                                    start=True, stop=True)
                ins.then_inc(pe_s1, 1)

            def values1(t):
                pe.wait_ge(p1_ready, t + 1)
                pe.wait_ge(v1_ready, t + 1)
                if t:
                    pe.wait_ge(o_norm, t)
                for i in range(I):
                    for g in range(G):
                        h = I * g + i
                        ins = pe.matmul(pv_psum[32 * g:32 * g + 32, i * G * V9:(i + 1) * G * V9],
                                        P1[t % 2][:, h, :], Vb1[t % 2][:, h, :, :].rearrange("p g v -> p (g v)"), start=True, stop=True)
                ins.then_inc(pe_pv, 1)

            issued = {"rope": 0, "out": 0, "turn": 0, "gate": 0, "count": 0}

            def bank0_free():
                pe.wait_ge(rope_mul, issued["rope"])
                if issued["out"]:
                    pe.wait_ge(normed, NT + CT * issued["out"])
                if issued["gate"]:
                    pe.wait_ge(gate_sub, issued["gate"])

            def bank1_free():
                pe.wait_ge(rope_mul, issued["rope"])
                if issued["turn"]:
                    pe.wait_ge(x2T_ready, issued["turn"])
                if issued["count"]:
                    pe.wait_ge(slot_ready, issued["count"])

            def project_out(cc):
                layer, c = divmod(cc, NC)
                pe.wait_ge(o_ready, CT * (cc + 1))
                if cc == 0:
                    pe.wait_ge(xb_ready, 1)
                    pe.wait_ge(ld_cst, 16)
                if layer:
                    bank0_free()
                    issued["out"] += 1
                elif c:
                    pe.wait_ge(normed, CT * c)
                res = x1T if layer else xb
                for t in range(cc * CT, (cc + 1) * CT):
                    i = t - layer * NT
                    pe.matmul(out_psum(t), OT[t % (2 * CT)][:, :], w2[:, 5, :] if layer else w1[:, 3, :], start=True, stop=False)
                    ins = pe.matmul(out_psum(t), res[:, i * T:(i + 1) * T], ident, start=False, stop=True)
                ins.then_inc(pe_out, 1)

            def turn1(c):
                if c:
                    pe.wait_ge(x1T_ready, c)
                for i in range(CT):
                    pe.wait_ge(normed, c * CT + i + 1)
                    pe.transpose(PSS[1][:, 1, i * T:(i + 1) * T], x1n[c % 2][:, i, :], ident).then_inc(pe_t1, 1)

            def rope(n):
                w, c = ROPES[n]
                if n == 0:
                    pe.wait_ge(ld_w2, 16)
                    pe.wait_ge(ld_ctx, 16)
                    pe.wait_ge(sp_lin, 2 * NC)
                else:
                    bank0_free()
                    bank1_free()
                issued["rope"] += 1
                if n == 1:
                    pe.wait_ge(x1T_ready, NC)
                src = (ctxT if w == "k" else x1T)[:, c * CH:(c + 1) * CH]
                base = 2 if w == "k" else 0
                pe.matmul(PS[0][:, :], w2[:, base, :], src, start=True, stop=True)
                pe.matmul(PS[1][:, :], w2[:, base + 1, :], src, start=True, stop=True).then_inc(pe_rope, 1)

            def values2_in(t):
                if t == 0:
                    pe.wait_ge(v1_ready, NT)
                else:
                    pe.wait_ge(v2_ready, t)
                for k in range(2):
                    base = ctxT[:, t * T + k * S:t * T + k * S + S]
                    for b in range(2):
                        keys = ctxT[:, t * T + b * B + k * S:t * T + b * B + k * S + S]
                        for q in range(2):
                            g = 2 * b + q
                            ins = pe.matmul(PS[2][32 * g:32 * g + 32, k * C:(k + 1) * C], keys, w2[:, 4, :], start=True, stop=True)
                ins.then_inc(pe_v2, 1)

            def scores2(t):
                c, i = divmod(t, CT)
                if t == 0:
                    pe.wait_ge(rows_ready, 2)
                if i == 0:
                    pe.wait_ge(rope_done, ROPES.index(("q", c)) + 1)
                    pe.wait_ge(widened[c % 2], 16 * H * ((NC + c) // 2 + 1))
                if t >= 2:
                    pe.wait_ge(sub_done, t - 1)
                if t == 1:
                    pe.wait_ge(o_norm, NT)
                    pe.wait_ge(x1T_ready, NC)
                for half in range(2):
                    for b in range(2):
                        a = t * T + b * B
                        pe.matmul(PSS[t % 2][64 * b:64 * b + 64, half, :], mrow[:, a:a + B],
                                  nrow[:, None, a:a + B].to_broadcast([128, H // 2, B]), start=True, stop=False)
                for half in range(2):
                    for b in range(2):
                        a = i * T + b * B
                        ins = pe.matmul(PSS[t % 2][64 * b:64 * b + 64, half, :], qT2[c % 2][:, a:a + B],
                                        wide[c % 2][:, half * 8:half * 8 + 8, a:a + B], start=False, stop=True)
                ins.then_inc(pe_s2, 1)

            def values2(t):
                pe.wait_ge(pt_ready, t + 1)
                pe.wait_ge(v2_ready, t + 1)
                if t:
                    pe.wait_ge(o_norm, NT + t)
                for i in range(I):
                    for k in range(2):
                        for g in range(G):
                            h = I * g + i
                            ins = pe.matmul(pv_psum[32 * g:32 * g + 32, i * G * V9:(i + 1) * G * V9], PT[t % 2][:, h, k, :],
                                            Vb2[t % 2][:, k, h, :, :].rearrange("p g v -> p (g v)"), start=(k == 0), stop=(k == 1))
                ins.then_inc(pe_pv, 1)

            def turn2(c):
                bank1_free()
                issued["turn"] += 1
                for i in range(CT):
                    t = c * CT + i
                    pe.wait_ge(normed, NT + t + 1)
                    ins = pe.transpose(PS[1][:, i * T:(i + 1) * T], xrow[:, t, 0, 0:C], ident)
                ins.then_inc(pe_t2, 1)

            def gate(c):
                if c == 0:
                    pe.wait_ge(ld_wg, 16)
                bank0_free()
                issued["gate"] += 1
                pe.wait_ge(x2T_ready, c + 1)
                for i in range(CT):
                    ins = pe.matmul(gate_psum[:, i * E:(i + 1) * E], x2T[:, i * T:(i + 1) * T], wg[:, :], start=True, stop=True)
                ins.then_inc(pe_gate, 1)

            def count(c):
                pe.wait_ge(mem_ready, c + 1)
                bank1_free()
                issued["count"] += 1
                if c == 0:
                    pe.wait_ge(ones_ready, 2)
                pe.matmul(cum_psum, tri[:, :], mem[:, :, :].rearrange("p t e -> p (t e)"), start=True, stop=True)
                for j in range(CT):
                    m = CT - j
                    ins = pe.matmul(cum_psum[:, (j + 1) * E:], ones[:, :], mem[:, j:j + 1, :].to_broadcast([128, m, E]),
                                    start=False, stop=True, skip_group_check=True)
                ins.then_inc(pe_cum, 1)

            project1(0)
            for k in range(NT + 8):
                if k % CT == 0 and k < NT:
                    project_v1(k // CT)
                if k % CT == 0 and k // CT + 1 < NC:
                    project1(k // CT + 1)
                if k < NT:
                    scores1(k)
                if 1 <= k <= NT:
                    values1(k - 1)
                if k >= 5 and (k - 5) % CT == 0 and (k - 5) // CT < NC:
                    project_out((k - 5) // CT)
                if k == NT - 2:
                    rope(0)
                if k >= 7 and (k - 7) % CT == 0 and (k - 7) // CT < NC:
                    turn1((k - 7) // CT)
            rope(1)
            for k in range(NT + 13):
                if k < NT:
                    scores2(k)
                    values2_in(k)
                if k % CT == 1 and k // CT + 1 < NC:
                    rope(2 * (k // CT + 1))
                if k % CT == 2 and k // CT + 1 < NC:
                    rope(2 * (k // CT + 1) + 1)
                if 1 <= k <= NT:
                    values2(k - 1)
                for off, step in ((12, count), (10, gate), (9, turn2), (7, lambda c: project_out(NC + c))):
                    if k >= off and (k - off) % CT == 0 and (k - off) // CT < NC:
                        step((k - off) // CT)

            def turn_rows(e):
                pe.wait_ge(et_in[e % 2], 16 * (e // 2 + 1))
                if e:
                    pe.wait_ge(xeT_ready, e)
                for j in range(CT):
                    ins = pe.transpose(PS[0][:, j * T:(j + 1) * T], et[e % 2][:, j, 0:C], ident)
                ins.then_inc(pe_te, 1)

            def hidden(e):
                if e == 0:
                    pe.wait_ge(ld_fc, 16)
                pe.wait_ge(xeT_ready, e + 1)
                if e >= 2:
                    pe.wait_ge(hid_ready, e - 1)
                pa, pg, pm = expert_psum(e)
                x = xeT[e % 2][:, :]
                pe.matmul(pa, fc[:, e, 0:128], x, start=True, stop=True)
                pe.matmul(pg, fc[:, e, 128:256], x, start=True, stop=True)
                pe.matmul(pm[0:64, :], fc[:, e, 256:320], x, start=True, stop=True)
                pe.matmul(pm[64:128, :], fc[:, e, 320:384], x, start=True, stop=True).then_inc(pe_h, 1)

            def expert_out(e):
                if e == 0:
                    pe.wait_ge(ld_pj, 32)
                else:
                    pe.wait_ge(ys_ready, CT * e)
                pe.wait_ge(hid_ready, e + 1)
                for j in range(CT):
                    o = PS7[:, j * C:(j + 1) * C]
                    pe.matmul(o, hid[e % 2][:, 0, j * T:(j + 1) * T], pj0[:, e, :], start=True, stop=False)
                    ins = pe.matmul(o, hid[e % 2][:, 1, j * T:(j + 1) * T], pj1[:, e, :], start=False, stop=True)
                ins.then_inc(pe_y, 1)

            turn_rows(0)
            for e in range(E):
                hidden(e)
                if e + 1 < E:
                    turn_rows(e + 1)
                expert_out(e)

        @block.vector
        def _(dve):
            chain = [0]

            def link(ins):
                chain[0] += 1
                ins.then_inc(dve_chain, 1)
                dve.wait_ge(dve_chain, chain[0])

            dve.memset(wide[0][:, :, :], 0.0).then_inc(z_wide[0], 1)
            link(dve.memset(Vb1[0][:, :, :, :], 0.0))
            link(dve.memset(Vb1[1][:, :, :, :], 0.0))
            for i in range(2):
                for g in range(G):
                    link(dve.memset(Vb1[i][32 * g:32 * g + 32, :, g, D:V9], 1.0))

            def softplus(c):
                for r in range(2):
                    n = 2 * c + r
                    dve.wait_ge(sp_exp, n + 1)
                    link(dve.tensor_scalar(wbuf[r][:, :], ebuf[r][:, :], 1.0, -1.0, ALU.add, ALU.add))
                    link(dve.tensor_tensor(wbuf[r][:, :], ebuf[r][:, :], wbuf[r][:, :], ALU.subtract))
                    dve.wait_ge(sp_ln, n + 1)
                    dve.wait_ge(sp_lin, n + 1)
                    link(dve.scalar_tensor_tensor(xlin[r][:, :], xlin[r][:, :], 0.0, lbuf[r][:, :], ALU.max, ALU.add))
                    if c >= 2 and r == 0:
                        dve.wait_ge(widened[c % 2], 16 * H * (c // 2))
                    if c >= 2 and r == 1:
                        dve.wait_ge(pe_s1, CT * (c - 1))
                    dst = (qT if r == 0 else kT)[c % 2]
                    dve.tensor_tensor(dst[:, :], xlin[r][:, :], wbuf[r][:, :], ALU.add).then_inc(sp_done, 1)

            def vb1(t):
                c, i = divmod(t, CT)
                dve.wait_ge(pe_v1, c + 1)
                if t == 0:
                    dve.wait_ge(ld_bv, 16)
                if t >= 2:
                    dve.wait_ge(pe_pv, t - 1)
                for g in range(G):
                    ps = slice(32 * g, 32 * g + 32)
                    ins = dve.tensor_tensor(Vb1[t % 2][ps, :, g, 0:D], PS[2][ps, i * C:(i + 1) * C].rearrange("p (h d) -> p h d", d=D),
                                            bvb[ps, :].rearrange("p (h d) -> p h d", d=D), ALU.add)
                ins.then_inc(v1_ready, 1)

            def causal(t):
                dve.wait_ge(pe_s1, t + 1)
                if t == 0:
                    dve.wait_ge(ld_cst, 16)
                if t >= 2:
                    dve.wait_ge(pe_pv, t - 1)
                dve.tensor_tensor(P1[t % 2][:, :, :], PSS[0][:, t % 2, :].rearrange("p (h s) -> p h s", s=S),
                                  cst[:, None, K_CAUSAL:K_CAUSAL + S].to_broadcast([128, H, S]), ALU.mult).then_inc(p1_ready, 1)

            def attn_out(t):
                dve.wait_ge(pe_pv, t + 1)
                pv = pv_psum.rearrange("p (i g v) -> p i g v", i=I, g=G)
                link(dve.reciprocal(rden[:, t % 2, :, :], pv[:, :, :, D]))
                dve.tensor_tensor(O[t % 2][:, :, :, :].rearrange("p g i d -> p i g d"), pv[:, :, :, 0:D],
                                  rden[:, t % 2, :, :, None].to_broadcast([128, I, G, D]), ALU.mult).then_inc(o_norm, 1)
                dve.wait_ge(o_norm, t + 1)
                if t >= 2 * CT:
                    dve.wait_ge(pe_out, t // CT - 1)
                dve.transpose(OT[t % (2 * CT)][:, :], O[t % 2][:, :, :, :].rearrange("p g i d -> p (g i d)")).then_inc(o_ready, 1)

            def moments(t, src):
                link(dve.bn_stats(stats[:, t, :], src))
                dve.bn_aggr(mv[:, t, :], stats[:, t, :]).then_inc(mv_ready, 1)

            def moments_out(c):
                dve.wait_ge(pe_out, c + 1)
                for t in range(c * CT, (c + 1) * CT):
                    moments(t, out_psum(t))

            def norm(c, src, dst):
                a, b = c * CT, (c + 1) * CT
                dve.wait_ge(r0_ready, c + 1)
                link(dve.tensor_tensor(r1[:, a:b], r0[:, a:b], r0[:, a:b], ALU.mult))
                link(dve.scalar_tensor_tensor(r1[:, a:b], mv[:, a:b, 1], EPS, r1[:, a:b], ALU.add, ALU.mult))
                link(dve.tensor_scalar(r1[:, a:b], r1[:, a:b], -0.5, 1.5, ALU.mult, ALU.add))
                link(dve.tensor_tensor(rstd[:, a:b], r1[:, a:b], r0[:, a:b], ALU.mult))
                for t in range(a, b):
                    d, s = dst(t), src(t)
                    dve.tensor_scalar(d, s, mv[:, t, 0:1], rstd[:, t:t + 1], ALU.subtract, ALU.mult).then_inc(normed, 1)

            def norm1(c):
                if c == 0:
                    dve.wait_ge(init_d, 16 * 2 * E)
                if c >= 2:
                    dve.wait_ge(pe_t1, CT * (c - 1))
                norm(c, out_psum, lambda t: x1n[c % 2][:, t % CT, :])

            def norm2(c):
                norm(NC + c, lambda t: out_psum(t)[:, None, :].to_broadcast([128, K2, C]), lambda t: xrow[:, t - NT, :, 0:C])

            softplus(0)
            for k in range(NT + 6):
                if k < NT:
                    vb1(k)
                    causal(k)
                if 1 <= k <= NT:
                    attn_out(k - 1)
                if k >= 5 and (k - 5) % CT == 0 and (k - 5) // CT < NC:
                    moments_out((k - 5) // CT)
                if k % CT == 0 and k // CT + 1 < NC:
                    softplus(k // CT + 1)
                if k == 2:
                    dve.memset(ones[:, :], 1.0).then_inc(ones_ready, 1)
                    dve.tensor_copy(tri[:, :], cst[:, K_TRI:K_TRI + 128]).then_inc(ones_ready, 1)
                    dve.memset(carry[0][:, :], 0.0)
                    dve.memset(mem[:, :, :], 0.0)
                    for i in range(2):
                        link(dve.memset(Vb2[i][:, :, :, :, :].rearrange("p k h g v -> p (k h g v)"), 0.0))
                        for g in range(G):
                            ins = dve.memset(Vb2[i][32 * g:32 * g + 32, :, :, g, D:V9], 1.0)
                        ins.then_inc(z_vb, 1)
                if k >= 6 and (k - 6) % CT == 0 and (k - 6) // CT < NC:
                    norm1((k - 6) // CT)
                if k == NT:
                    rope_products(dve, 0)

            def maxsub(t):
                dve.wait_ge(pe_s2, t + 1)
                link(dve.tensor_reduce(mx2[:, t % 2, :], PSS[t % 2][:, :, :].rearrange("p a (h b) -> p (a h) b", b=B), AX.X, ALU.max))
                if t >= 2:
                    dve.wait_ge(pt_ready, t - 1)
                dve.tensor_tensor(SC[t % 2][:, :, :], PSS[t % 2][:, :, :].rearrange("p a (h b) -> p (a h) b", b=B),
                                  mx2[:, t % 2, :, None].to_broadcast([128, H, B]), ALU.subtract).then_inc(sub_done, 1)

            def turn_probs(t):
                dve.wait_ge(exp_done, t + 1)
                if t >= 2:
                    dve.wait_ge(pe_pv, NT + t - 1)
                dve.transpose(PT[t % 2][:, :, :, :].rearrange("p h k s -> p (h k s)"), SC[t % 2][:, :, :].rearrange("p h b -> p (h b)")).then_inc(pt_ready, 1)

            def route_a(c):
                dve.wait_ge(pe_gate, c + 1)
                p = gate_psum.rearrange("p (t e) -> p t e", e=E)
                link(dve.tensor_reduce(g1[:, :], p, AX.X, ALU.max))
                dve.tensor_tensor(gl[:, :, :], p, g1[:, :, None].to_broadcast([128, CT, E]), ALU.subtract).then_inc(gate_sub, 1)

            def route_b(c):
                dve.wait_ge(gate_exp, c + 1)
                link(dve.tensor_reduce(g1[:, :], ge[:, :, :], AX.X, ALU.add))
                link(dve.reciprocal(g1[:, :], g1[:, :]))
                link(dve.tensor_tensor(gs[:, :, :], ge[:, :, :], g1[:, :, None].to_broadcast([128, CT, E]), ALU.mult))
                rank = cst[:, None, K_RANK:K_RANK + E].to_broadcast([128, CT, E])
                for k in range(K2):
                    link(dve.tensor_reduce(gm[:, k, :], gs[:, :, :], AX.X, ALU.max))
                    link(dve.tensor_tensor(gt[:, :, :], gs[:, :, :], gm[:, k, :, None].to_broadcast([128, CT, E]), ALU.is_equal))
                    link(dve.tensor_tensor(gt[:, :, :], gt[:, :, :], rank, ALU.mult))
                    link(dve.tensor_reduce(g1[:, :], gt[:, :, :], AX.X, ALU.max))
                    link(dve.tensor_tensor(pick[:, k, :, :], rank, g1[:, :, None].to_broadcast([128, CT, E]), ALU.is_equal))
                    if k == 0:
                        link(dve.scalar_tensor_tensor(gs[:, :, :], pick[:, 0, :, :], -2.0, gs[:, :, :], ALU.mult, ALU.add))
                if c:
                    dve.wait_ge(pe_cum, c)
                dve.tensor_tensor(mem[:, 0:CT, :], pick[:, 0, :, :], pick[:, 1, :, :], ALU.add).then_inc(mem_ready, 1)
                dve.tensor_copy(xrow[:, c * CT:(c + 1) * CT, :, C + 1].rearrange("p t k -> p k t"), gm[:, :, :])

            def route_c(c):
                dve.wait_ge(pe_cum, c + 1)
                cum = cum_psum.rearrange("p (t e) -> p t e", e=E)
                link(dve.tensor_tensor(pos[:, :, :], cum[:, 0:CT, :], carry[c % 2][:, None, :].to_broadcast([128, CT, E]), ALU.add))
                dve.tensor_tensor(carry[(c + 1) % 2][:, :], cum[:, CT, :], carry[c % 2][:, :], ALU.add)
                for k in range(K2):
                    link(dve.tensor_tensor(pp[:, k, :, :], pos[:, :, :], pick[:, k, :, :], ALU.mult))
                    link(dve.tensor_tensor(pq[:, k, :, :], pick[:, k, :, :], cst[:, None, K_BASE:K_BASE + E].to_broadcast([128, CT, E]), ALU.mult))
                link(dve.tensor_reduce(psel[:, :, :], pp[:, :, :, :], AX.X, ALU.add))
                link(dve.tensor_reduce(bsel[:, :, :], pq[:, :, :, :], AX.X, ALU.add))
                link(dve.tensor_scalar(over[:, :, :], psel[:, :, :], float(CAP), UNUSED, ALU.is_ge, ALU.mult))
                link(dve.tensor_tensor(psel[:, :, :], psel[:, :, :], bsel[:, :, :], ALU.add))
                dve.tensor_tensor(slot[:, c * CT:(c + 1) * CT, :].rearrange("p t k -> p k t"), psel[:, :, :], over[:, :, :], ALU.add).then_inc(slot_ready, 1)

            rope_products(dve, 1)
            dve.wait_ge(ld_dest, 16)
            dve.tensor_copy(xrow[:, :, :, C].bitcast(U32), dest[:, :, :])
            for k in range(NT + 13):
                if k < NT:
                    maxsub(k)
                if 2 <= k <= NT + 1:
                    attn_out(NT + k - 2)
                if 1 <= k <= NT:
                    turn_probs(k - 1)
                if k % CT == 1 and k // CT + 1 < NC:
                    rope_products(dve, 2 * (k // CT + 1))
                if k % CT == 2 and k // CT + 1 < NC:
                    rope_products(dve, 2 * (k // CT + 1) + 1)
                for off, step in ((10, route_a), (7, lambda c: moments_out(NC + c)), (8, norm2), (11, route_b), (12, route_c)):
                    if k >= off and (k - off) % CT == 0 and (k - off) // CT < NC:
                        step((k - off) // CT)

            dve.wait_ge(pe_pv, 2 * NT)
            for i in range(2):
                link(dve.memset(hid[i][0:64, 1, :], 0.0))
            for e in range(E):
                pa, pg, pm = expert_psum(e)
                dve.wait_ge(sil_ready, e + 1)
                if e >= 2:
                    dve.wait_ge(pe_y, e - 1)
                dve.tensor_tensor(hid[e % 2][:, 0, :], sil[e % 2][:, 0, :], pg, ALU.mult)
                dve.tensor_tensor(hid[e % 2][64:128, 1, :], sil[e % 2][64:128, 1, :], pm[64:128, :], ALU.mult).then_inc(hid_ready, 1)

            for c in range(NC + 1):
                if c < NC:
                    dve.wait_ge(y_sum, c + 1)
                    a, b = c * CT, (c + 1) * CT
                    link(dve.tensor_tensor(Z[:, a:b, :], Z[:, a:b, :], xrow[:, a:b, 0, 0:C], ALU.add))
                    for t in range(a, b):
                        moments(2 * NT + t, Z[:, t, :])
                if c:
                    norm(2 * NC + c - 1, lambda t: Z[:, t - 2 * NT, :], lambda t: R[:, t - 2 * NT, :])


def _lay_out(i):
    f = lambda n: np.asarray(i[n])
    swap = np.arange(C) ^ 1
    wq, wkv = f("L0_xattn_W_q"), f("L0_xattn_W_kv")
    wk, wv = wkv[:, :C], wkv[:, C:]
    fc = f("L0_ffn_c_fc")
    fc = np.concatenate([fc[:, :, 0:128], fc[:, :, F:F + 128], fc[:, :, 128:F], fc[:, :, F + 128:]], axis=2)
    k, dest, blank = constants()
    return {
        "xT": np.ascontiguousarray(f("x").transpose(2, 1, 0).reshape(C, N)),
        "ctxT": np.ascontiguousarray(f("ctx_1024").transpose(2, 0, 1).reshape(C, N)),
        "mask": np.ascontiguousarray(f("mask_BxS2_bf1").reshape(1, N)).view(np.uint8),
        "cols": np.stack([np.repeat(f("L0_attn_beta"), D), f("L0_attn_bq"), f("L0_attn_bk"), f("L0_attn_bo")], axis=1),
        "bv": f("L0_attn_bv").reshape(1, C),
        "w1": np.concatenate([f(n).T for n in ("L0_attn_Wq", "L0_attn_Wk", "L0_attn_Wv", "L0_attn_Wo")], axis=1),
        "w2": np.concatenate([wq, wq[:, swap], wk, wk[:, swap], wv, f("L0_xattn_W_c")], axis=1),
        "wg": f("L0_ffn_w_gate"),
        "fc": np.ascontiguousarray(fc.transpose(1, 0, 2).reshape(C, E * 2 * F)),
        "proj": f("L0_ffn_c_proj"),
        "consts": k, "dest": dest, "blank": blank,
    }


def kernel(**inputs):
    import concourse.bacc as bacc
    from concourse.bass_utils import run_bass_kernel_spmd

    nc = bacc.Bacc("TRN2", target_bir_lowering=False, num_devices=1)
    arrays, args = {}, []
    for name, a in _lay_out(inputs).items():
        a = np.ascontiguousarray(a)
        arrays[f"in_{name}"] = a
        args.append(nc.dram_tensor(f"in_{name}", a.shape, mybir.dt.from_np(a.dtype), kind="ExternalInput").ap())
    out = nc.dram_tensor("out_0", (S, B, C), F32, kind="ExternalOutput").ap()
    decoder_layer(nc, *args, out)
    r = run_bass_kernel_spmd(nc, [arrays], core_ids=[0])
    return r.results[0]["out_0"]
```

```python
from contextlib import ExitStack

import numpy as np

import concourse.bass as bass
from concourse import mybir

ALU = mybir.AluOpType
ACT = mybir.ActivationFunctionType
AX = mybir.AxisListType
F32 = mybir.dt.float32
BF16 = mybir.dt.bfloat16
U32 = mybir.dt.uint32
U8 = mybir.dt.uint8

S, B, C = 32, 64, 128
N = S * B
H, D = 16, 8
T = 128
NT = N // T
CT = 4
CH = CT * T
NC = N // CH
G = 4
I = H // G
V9 = D + 1
E, K2, CAP = 8, 2, 512
F = 192
FR = F - 128
ROW = C + 2
EPS = 1e-5
POOL_HEADS, ACT_HEADS, DMA_HEADS = range(0, 6), range(6, 11), range(11, H)
YS = 6
POOL_SINES = 3
PAIR = [i ^ 1 for i in range(32)]
UNUSED = 1e6

K_ID, K_TRI, K_CAUSAL = 0, 128, 256
K_COSQ, K_SINQ, K_COSK, K_SINK = 288, 352, 416, 480
K_RANK, K_BASE, K_COEF, K_HEAD = 544, 552, 560, 564
K_COLS = K_HEAD + H


def constants():
    k = np.zeros((128, K_COLS), np.float32)
    k[:, K_ID:K_ID + 128] = np.eye(128)
    k[:, K_TRI:K_TRI + 128] = np.triu(np.ones((128, 128)), 1)
    s = np.arange(S)
    k[:, K_CAUSAL:K_CAUSAL + S] = (s[None, :] >= (np.arange(128) % S)[:, None])
    w = (1.0 / np.float32(10000.0) ** (np.arange(1, D + 1, 2, dtype=np.float32) / np.float32(D))).astype(np.float32)
    angle = np.arange(1, B + 1, dtype=np.float32)[None, :] * w[(np.arange(C) % D) // 2][:, None]
    sign = np.where(np.arange(C) % 2 == 0, -1.0, 1.0)[:, None]
    scale = 1.0 / np.sqrt(np.float64(D))
    k[:, K_COSQ:K_COSQ + B] = np.cos(angle) * scale
    k[:, K_SINQ:K_SINQ + B] = np.sin(angle) * sign * scale
    k[:, K_COSK:K_COSK + B] = np.cos(angle)
    k[:, K_SINK:K_SINK + B] = np.sin(angle) * sign
    k[:, K_RANK:K_RANK + E] = E - np.arange(E)
    k[:, K_BASE:K_BASE + E] = CAP * np.arange(E)
    rest = np.float64(-1e9)
    for r in range(3):
        bits = np.array([rest], np.float32).view(np.uint32) & np.uint32(0xFFFF0000)
        part = bits.view(np.float32)[0]
        k[r, K_COEF:K_COEF + 3] = (1.0, part, -part)
        rest -= np.float64(part)
    assert rest == 0
    k[:, K_COEF + 3] = EPS
    k[:, K_HEAD:K_HEAD + H] = (np.arange(C)[:, None] // D == np.arange(H)[None, :])
    dest = (np.arange(NT)[None, :, None] * T + np.arange(T)[:, None, None] + N * np.arange(K2)[None, None, :])
    blank = np.zeros((128, 4, ROW), np.float32)
    blank.view(np.uint32)[:, :, C] = int(UNUSED)
    return k, dest.astype(np.uint32).reshape(128, NT * K2), blank.reshape(128, 4 * ROW)


def decoder_layer(nc, xT_d, ctxT_d, mask_d, cols_d, w1_d, w2_d, wg_d, fc_d, proj_d, const_d, dest_d, blank_d, out):
    with ExitStack() as ctx:
        def sb(name, shape, dt=F32):
            return ctx.enter_context(nc.sbuf_tensor(name, shape, dt))

        def sem(name):
            return ctx.enter_context(nc.semaphore(name))

        slots_d = nc.dram_tensor("slots_d", (E * CAP, ROW), F32, kind="Internal").ap()
        picks_d = nc.dram_tensor("picks_d", (K2 * N, C), F32, kind="Internal").ap()

        xT = sb("xT", [128, N])
        ctxT = sb("ctxT", [128, N])
        x1T = sb("x1T", [128, N])
        w1 = sb("w1", [128, 4, 128])
        w2 = sb("w2", [128, 4, 128])
        wg = sb("wg", [128, E])
        fc = sb("fc", [128, E, 2 * F])
        pj0 = sb("pj0", [128, E, C])
        pj1 = sb("pj1", [128, E, C])
        cst = sb("cst", [128, K_COLS])
        cols = sb("cols", [128, 5])
        scol = sb("scol", [128, 4])
        obias = sb("obias", [128, 1])
        dest = sb("dest", [128, NT, K2], U32)
        tri = sb("tri", [128, 128], BF16)
        ones = sb("ones", [128, 128], BF16)
        mask8 = sb("mask8", [128, N], U8)
        cosq = sb("cosq", [128, N])
        sinq = sb("sinq", [128, N])
        mrow = sb("mrow", [128, N], BF16)
        nrow = sb("nrow", [128, N], BF16)
        wide = [sb(f"wide{i}", [128, H, CH]) for i in range(2)]
        soft = sb("soft", [128, 8, CH])
        work = sb("work", [128, 4, CH])
        early = sb("early", [128, N + 2 * CH + 2 * H * G * V9])
        Vb2 = [sb(f"Vb2_{i}", [128, 2, H, G, V9]) for i in range(2)]
        x1pair = sb("x1pair", [128, 2, CT, C])
        x1n = [x1pair[:, i, :, :] for i in range(2)]
        x2T = sb("x2T", [128, CH])
        rden = sb("rden", [128, 2, I, G])
        O = [sb(f"O{i}", [128, G, I, D]) for i in range(2)]
        OT = [sb(f"OT{i}", [128, T]) for i in range(2 * CT)]
        stats = sb("stats", [128, 3 * NT, 6])
        mv = sb("mv", [128, 3 * NT, 2])
        lnv = sb("lnv", [128, 3 * NT])
        r0 = sb("r0", [128, 3 * NT])
        r1 = sb("r1", [128, 3 * NT])
        rstd = sb("rstd", [128, 3 * NT])
        shift = sb("shift", [128, NT])
        mx2 = sb("mx2", [128, 2, H])
        xlin, ebuf, lbuf, wbuf = ([soft[:, 2 * n + i, :] for i in range(2)] for n in range(4))
        qT, kT = ([work[:, 2 * n + i, :] for i in range(2)] for n in range(2))
        xb = early[:, 0:N]
        P1 = [early[:, N + i * CH:N + (i + 1) * CH].rearrange("p (h s) -> p h s", s=S) for i in range(2)]
        Vb1 = [early[:, N + 2 * CH + i * H * G * V9:N + 2 * CH + (i + 1) * H * G * V9]
               .rearrange("p (h g v) -> p h g v", h=H, g=G) for i in range(2)]
        xrow = early[:, 0:NT * K2 * ROW].rearrange("p (t k n) -> p t k n", t=NT, k=K2)
        maskf = sinq
        blank_sb, zero_sb = cosq[:, 0:4 * ROW], cosq[:, 5 * ROW:5 * ROW + 4 * C]
        qT2, kT2 = ([xT[:, (2 * n + i) * CH:(2 * n + i + 1) * CH] for i in range(2)] for n in range(2))
        ra, rb = xlin, ebuf
        SC = [soft[:, 4 + 2 * i:6 + 2 * i, :].rearrange("p a (h b) -> p (a h) b", b=B) for i in range(2)]
        PT = [work[:, 2 * i:2 * i + 2, :].rearrange("p a (h k s) -> p (a h) k s", k=2, s=S) for i in range(2)]
        flat = [wide[i][:, :, :].rearrange("p h n -> p (h n)")[:, 8 * CH:] for i in range(2)]
        et = [flat[e % 2][:, (e // 2) * CT * ROW:(e // 2 + 1) * CT * ROW].rearrange("p (j n) -> p j n", j=CT) for e in range(E)]
        ys = [flat[e % 2][:, (5 + e // 2) * CT * C:(6 + e // 2) * CT * C].rearrange("p (j n) -> p j n", j=CT) for e in range(YS)]
        xeT = xlin
        sil = [soft[:, 4 + 2 * i:6 + 2 * i, :] for i in range(2)]
        hid = [work[:, 2 * i:2 * i + 2, :] for i in range(2)]
        gl = sb("gl", [128, CT, E])
        ge = sb("ge", [128, CT, E])
        gs = sb("gs", [128, CT, E])
        g1 = sb("g1", [128, CT])
        gm = sb("gm", [128, K2, CT])
        gt = sb("gt", [128, CT, E])
        pick = sb("pick", [128, K2, CT, E])
        mem = sb("mem", [128, CT + 1, E], BF16)
        carry = [sb(f"carry{i}", [128, E]) for i in range(2)]
        pos = sb("pos", [128, CT, E])
        pp = sb("pp", [128, K2, CT, E])
        psel = sb("psel", [128, K2, CT])
        over = sb("over", [128, CT, E])
        slot = sb("slot", [128, NT, K2], U32)
        Y = [wide[i][:, 0:4, :].rearrange("p a (t c) -> p (a t) c", c=C) for i in range(2)]
        Z = wide[0][:, 4:8, :].rearrange("p a (t c) -> p (a t) c", c=C)
        R = wide[1][:, 4:8, :].rearrange("p a (t c) -> p (a t) c", c=C)

        PS = [ctx.enter_context(nc.psum_tensor(f"PS{i}", [128, 512], F32)) for i in range(3)]
        PSS = [ctx.enter_context(nc.psum_tensor(f"PSS{i}", [128, 2, 512], F32)) for i in range(2)]
        PS7 = ctx.enter_context(nc.psum_tensor("PS7", [128, 512], F32))

        ld_x = [sem(f"ld_x{c}") for c in range(NC)]
        ld_w1, ld_cst, ld_cols = sem("ld_w1"), sem("ld_cst"), sem("ld_cols")
        pe_bias, bias_ready = sem("pe_bias"), sem("bias_ready")
        ld_ctx, ld_w2, ld_mask, ld_dest = sem("ld_ctx"), sem("ld_w2"), sem("ld_mask"), sem("ld_dest")
        ld_wg, ld_fc, ld_pj, ld_blank = sem("ld_wg"), sem("ld_fc"), sem("ld_pj"), sem("ld_blank")
        z_wide = [sem(f"z_wide{i}") for i in range(2)]
        z_small, z_cos, z_vb, z_vb1 = sem("z_small"), sem("z_cos"), sem("z_vb"), sem("z_vb1")
        init_d = sem("init_d")
        widened = [sem(f"widened{i}") for i in range(2)]
        wide_pool, wide_act = sem("wide_pool"), sem("wide_act")
        t_ready = sem("t_ready")
        rope_cos, rope_sin = sem("rope_cos"), sem("rope_sin")
        act_chain, dve_chain, pool_chain = sem("act_chain"), sem("dve_chain"), sem("pool_chain")
        sc_ready, xb_ready = sem("sc_ready"), sem("xb_ready")
        tabs_ready, rows_ready, ones_ready = sem("tabs_ready"), sem("rows_ready"), sem("ones_ready")
        pe_qk, pe_v1, pe_s1, pe_pv, pe_out, pe_t1 = (sem(n) for n in ("pe_qk", "pe_v1", "pe_s1", "pe_pv", "pe_out", "pe_t1"))
        sp_abs, sp_lin, sp_exp, sp_ln, sp_done = (sem(n) for n in ("sp_abs", "sp_lin", "sp_exp", "sp_ln", "sp_done"))
        p1_ready, v1_ready = sem("p1_ready"), sem("v1_ready")
        rden_ready, o_norm, o_ready = sem("rden_ready"), sem("o_norm"), sem("o_ready")
        max_ready = sem("max_ready")
        mv_ready, r0_ready, normed = sem("mv_ready"), sem("r0_ready"), sem("normed")
        x1T_ready = sem("x1T_ready")
        pe_rope, rope_mul, rope_done = sem("pe_rope"), sem("rope_mul"), sem("rope_done")
        pe_v2, v2_ready, pe_s2, sub_done, exp_done, pt_ready = (
            sem(n) for n in ("pe_v2", "v2_ready", "pe_s2", "sub_done", "exp_done", "pt_ready"))
        pe_t2, x2T_ready, pe_gate, gate_sub, gate_exp, mem_ready, pe_cum, slot_ready = (
            sem(n) for n in ("pe_t2", "x2T_ready", "pe_gate", "gate_sub", "gate_exp", "mem_ready", "pe_cum", "slot_ready"))
        scattered = sem("scattered")
        et_in = [sem(f"et_in{e}") for e in range(E)]
        pe_te, xeT_ready, pe_h, sil_ready, hid_ready, pe_y, ys_ready = (
            sem(n) for n in ("pe_te", "xeT_ready", "pe_h", "sil_ready", "hid_ready", "pe_y", "ys_ready"))
        picked = [sem(f"picked{e}") for e in range(E)]
        y_in = [sem(f"y_in{c}") for c in range(NC)]
        shift_ready, last_half = sem("shift_ready"), sem("last_half")
        y_sum, stored = sem("y_sum"), sem("stored")

        def col(a, b=None):
            return cst[:, a:(a + 1 if b is None else b)]

        ident = cst[:, K_ID:K_ID + 128]
        ROPES = [("k", 0), ("k", 1), ("q", 0), ("q", 1)] + [(w, c) for c in range(2, NC) for w in "kq"]

        def out_psum(t):
            return (PSS[1][:, 0, :] if t < NT else PS[0])[:, (t % CT) * 128:(t % CT) * 128 + 128]

        pv_psum = PS7[:, 0:I * G * V9]
        gate_psum = PS[1][:, (CT + 1) * E:(2 * CT + 1) * E]
        cum_psum = PS[1][:, 0:(CT + 1) * E]

        def scatter(pool, c):
            if c == 0:
                pool.wait_ge(init_d, 16 * 2 * E)
            pool.wait_ge(slot_ready, c + 1)
            pool.wait_ge(normed, NT + CT * (c + 1))
            for t in range(c * CT, (c + 1) * CT):
                for k in range(K2):
                    pool.indirect_dma_start(out=slots_d, out_offset=bass.IndirectOffsetOnAxis(ap=slot[:, t, k:k + 1], axis=0),
                                            in_=xrow[:, t, k, :], in_offset=None,
                                            bounds_check=E * CAP - 1, oob_is_err=False).then_inc(scattered, 16)

        def widened_dma(u):
            return 16 * len(DMA_HEADS) * (u // 2 + 1)

        def widen_wait(eng, u):
            if u < NC:
                eng.wait_ge(sp_done, 2 * u + 1)
            else:
                eng.wait_ge(rope_done, ROPES.index(("k", u - NC)) + 1)
            if 2 <= u < NC + 2:
                eng.wait_ge(pe_s1, CT * (u - 1))
            elif u >= NC + 2:
                eng.wait_ge(pe_s2, CT * (u - 1 - NC))

        def narrow(u):
            return (qT if u < NC else kT2)[u % 2]

        def widen_pool(pool, u):
            widen_wait(pool, u)
            for h in POOL_HEADS:
                ins = pool.tensor_scalar(wide[u % 2][:, h, :], narrow(u)[:, :], col(K_HEAD + h), 0.0, ALU.mult, ALU.add)
            ins.then_inc(wide_pool, 1)

        def widen_act(act, u):
            widen_wait(act, u)
            for h in ACT_HEADS:
                ins = act.activation(wide[u % 2][:, h, :], narrow(u)[:, :], ACT.Copy, scale=col(K_HEAD + h))
            ins.then_inc(wide_act, 1)

        def weigh(act, e):
            act.wait_ge(pe_y, e + 1)
            if e >= YS:
                act.wait_ge(picked[e - YS], 16 * CT)
            for j in range(CT):
                act.activation(ys[e % YS][:, j, :], PS7[:, j * C:(j + 1) * C], ACT.Copy,
                               scale=et[e][:, j, C + 1:C + 2]).then_inc(ys_ready, 1)

        def expert_psum(e):
            if e % 2:
                return PSS[1][:, 0, :], PSS[1][:, 1, :], PS[1][:, :]
            return PSS[0][:, 0, :], PSS[0][:, 1, :], PS[2][:, :]

        def routed(k):
            return [c for c in range(NC) if k == CT * c + (12 if c == NC - 2 else 13)]

        def by_s(ap):
            return ap[:, :].rearrange("p (s b) -> p s b", b=B)

        def rope_table(w, c, key_col, q_tab):
            if w == "k":
                return cst[:, None, key_col:key_col + B].to_broadcast([128, CH // B, B])
            return by_s(q_tab[:, c * CH:(c + 1) * CH])

        def rope_products(dve, n):
            w, c = ROPES[n]
            dve.wait_ge(pe_rope, n + 1)
            if ROPES[n] == ("q", 0):
                dve.wait_ge(tabs_ready, 2)
            if n >= 2:
                dve.wait_ge(rope_done, n - 1)
            dve.stream_shuffle(rb[n % 2][:, :], PS[1][:, :], PAIR).then_inc(rope_cos, 1)
            dve.tensor_tensor(by_s(ra[n % 2]), by_s(PS[1]), rope_table(w, c, K_COSK, cosq), ALU.mult).then_inc(rope_mul, 1)
            if n < POOL_SINES:
                dve.wait_ge(rope_cos, n + 1)
                dve.tensor_tensor(by_s(rb[n % 2]), by_s(rb[n % 2]), rope_table(w, c, K_SINK, sinq), ALU.mult).then_inc(rope_sin, 1)

        def due(k, off):
            return [(k - off) // CT] if k >= off and (k - off) % CT == 0 and (k - off) // CT < NC else []

        block = ctx.enter_context(nc.Block())

        @block.sync
        def _(sp):
            sp.dma_start(w1[:, :, :], w1_d.rearrange("p (a n) -> p a n", a=4)).then_inc(ld_w1, 16)
            for c in range(NC):
                sp.dma_start(xT[:, c * CH:(c + 1) * CH], xT_d[:, c * CH:(c + 1) * CH]).then_inc(ld_x[c], 16)
            sp.dma_start(ctxT[:, :], ctxT_d).then_inc(ld_ctx, 16)
            sp.dma_start(w2[:, :, :], w2_d.rearrange("p (a n) -> p a n", a=4)).then_inc(ld_w2, 16)

            def widen(u):
                widen_wait(sp, u)
                if u < 2:
                    sp.wait_ge(z_wide[u], 1)
                for h in DMA_HEADS:
                    sp.dma_start(wide[u % 2][D * h:D * h + D, h, :], narrow(u)[D * h:D * h + D, :]).then_inc(widened[u % 2], 16)

            for u in range(2 * NC):
                widen(u)
                if u == 0:
                    sp.dma_start(fc[:, :, :], fc_d.rearrange("p (e f) -> p e f", e=E)).then_inc(ld_fc, 16)
                    sp.dma_start(pj0[:, :, :], proj_d[:, 0:128, :].rearrange("e p n -> p e n")).then_inc(ld_pj, 16)
                    sp.wait_ge(z_small, 1)
                    sp.dma_start(pj1[64:128, :, :], proj_d[:, 128:F, :].rearrange("e p n -> p e n")).then_inc(ld_pj, 16)
                    sp.dma_start(wg[:, :], wg_d).then_inc(ld_wg, 16)
            sp.wait_ge(scattered, 16 * NT * K2)
            for e in range(E):
                sp.dma_start(et[e][:, :, :], slots_d[e * CAP:(e + 1) * CAP, :].rearrange("(p j) n -> p j n", j=CT)).then_inc(et_in[e], 16)
            for e in range(E):
                sp.wait_ge(picked[e], 16 * CT)
            for c in range(NC):
                for k in range(K2):
                    sp.dma_start(Y[k][:, c * CT:(c + 1) * CT, :],
                                 picks_d[k * N + c * CH:k * N + (c + 1) * CH, :].rearrange("(t p) n -> p t n", p=T)).then_inc(y_in[c], 16)
            out_v = out.rearrange("s b n -> (s b) n").rearrange("(t p) n -> p t n", p=T)
            for c in range(NC):
                if c < NC - 1:
                    sp.wait_ge(normed, 2 * NT + CT * (c + 1))
                else:
                    sp.wait_ge(normed, 3 * NT - CT // 2)
                    sp.wait_ge(last_half, CT // 2)
                sp.dma_start(out_v[:, c * CT:(c + 1) * CT, :], R[:, c * CT:(c + 1) * CT, :]).then_inc(stored, 16)
            sp.wait_ge(stored, 16 * NC)

        @block.gpsimd
        def _(pool):
            chain = [0]

            def link(ins):
                chain[0] += 1
                ins.then_inc(pool_chain, 1)
                pool.wait_ge(pool_chain, chain[0])

            first, last = DMA_HEADS[0], DMA_HEADS[-1] + 1
            pool.memset(wide[0][:, first:last, :], 0.0).then_inc(z_wide[0], 1)
            pool.wait_ge(ld_cst, 16)

            def softplus_rest(c):
                for r in range(2):
                    n = 2 * c + r
                    pool.wait_ge(sp_exp, n + 1)
                    pool.wait_ge(sp_done, n - 1)
                    link(pool.tensor_scalar(wbuf[r][:, :], ebuf[r][:, :], 1.0, 1.0, ALU.mult, ALU.add))
                    link(pool.tensor_scalar(wbuf[r][:, :], wbuf[r][:, :], -1.0, 1.0, ALU.mult, ALU.add))
                    pool.tensor_tensor(wbuf[r][:, :], ebuf[r][:, :], wbuf[r][:, :], ALU.add).then_inc(t_ready, 1)

            widen_pool(pool, 0)
            pool.memset(zero_sb[:, :], 0.0).then_inc(z_cos, 1)
            pool.memset(pj1[:, :, :], 0.0).then_inc(z_small, 1)
            pool.memset(wide[1][:, first:last, :], 0.0).then_inc(z_wide[1], 1)
            softplus_rest(1)
            widen_pool(pool, 1)
            pool.wait_ge(bias_ready, 1)
            for c in range(NC):
                pool.wait_ge(ld_x[c], 16)
            pool.tensor_scalar(xb[:, :], xT[:, :], obias[:, 0:1], 1.0, ALU.add, ALU.mult).then_inc(xb_ready, 1)
            softplus_rest(2)
            widen_pool(pool, 2)
            pool.wait_ge(ld_mask, 16)
            link(pool.tensor_scalar(maskf[:, :], mask8[:, :], 1.0, 0.0, ALU.mult, ALU.add))
            pool.tensor_scalar(mrow[:, :], maskf[:, :], col(K_COEF), 0.0, ALU.mult, ALU.add).then_inc(rows_ready, 1)
            pool.tensor_scalar(nrow[:, :], maskf[:, :], col(K_COEF + 2), col(K_COEF + 1), ALU.mult, ALU.add).then_inc(rows_ready, 1)
            softplus_rest(3)
            widen_pool(pool, 3)
            pool.wait_ge(init_d, 16 * 2 * E)
            m3 = maskf[:, :].rearrange("p (s b) -> p s b", b=B)
            for tab, k in ((cosq, K_COSQ), (sinq, K_SINQ)):
                pool.tensor_tensor(tab[:, :].rearrange("p (s b) -> p s b", b=B), m3,
                                   cst[:, None, k:k + B].to_broadcast([128, S, B]), ALU.mult).then_inc(tabs_ready, 1)

            def rope_sum(n):
                w, c = ROPES[n]
                if n >= POOL_SINES:
                    pool.wait_ge(rope_cos, n + 1)
                    pool.tensor_tensor(by_s(rb[n % 2]), by_s(rb[n % 2]), rope_table(w, c, K_SINK, sinq), ALU.mult).then_inc(rope_sin, 1)
                pool.wait_ge(rope_mul, n + 1)
                pool.wait_ge(rope_sin, n + 1)
                if c >= 2 and w == "k":
                    pool.wait_ge(widened[c % 2], widened_dma(NC + c - 2))
                    pool.wait_ge(wide_act, NC + c - 1)
                if c >= 2 and w == "q":
                    pool.wait_ge(pe_s2, CT * (c - 1))
                dst = kT2[c % 2] if w == "k" else qT2[c % 2]
                pool.tensor_tensor(dst[:, :], ra[n % 2][:, :], rb[n % 2][:, :], ALU.add).then_inc(rope_done, 1)

            for n, (w, c) in enumerate(ROPES):
                rope_sum(n)
                if w == "k":
                    widen_pool(pool, NC + c)
            for c in range(NC):
                scatter(pool, c)
            for e in range(E):
                for j in range(CT):
                    pool.wait_ge(ys_ready, CT * e + j + 1)
                    pool.indirect_dma_start(out=picks_d, out_offset=bass.IndirectOffsetOnAxis(ap=et[e][:, j, C:C + 1].bitcast(U32), axis=0),
                                            in_=ys[e % YS][:, j, :], in_offset=None,
                                            bounds_check=K2 * N - 1, oob_is_err=False).then_inc(picked[e], 16)
            for c in range(NC):
                pool.wait_ge(y_in[c], 32)
                pool.tensor_tensor(Z[:, c * CT:(c + 1) * CT, :], Y[0][:, c * CT:(c + 1) * CT, :], Y[1][:, c * CT:(c + 1) * CT, :], ALU.add).then_inc(y_sum, 1)

        @block.scalar
        def _(act):
            chain = [0]

            def link(ins):
                chain[0] += 1
                ins.then_inc(act_chain, 1)
                act.wait_ge(act_chain, chain[0])

            act.dma_start(cols[:, :], cols_d).then_inc(ld_cols, 16)
            act.dma_start(cst[:, :], const_d).then_inc(ld_cst, 16)
            act.dma_start(mask8[:, :], mask_d.to_broadcast([128, N])).then_inc(ld_mask, 16)
            act.dma_start(blank_sb[:, :], blank_d).then_inc(ld_blank, 16)
            act.dma_start(dest[:, :, :], dest_d.rearrange("p (t k) -> p t k", k=K2)).then_inc(ld_dest, 16)
            act.preload_act_table_set("natural_log_exp_and_others")
            act.wait_ge(ld_cols, 16)
            link(act.activation(scol[:, 3:4], cols[:, 0:1], ACT.Exp, scale=-1.0))
            link(act.mul(scol[:, 0:1], scol[:, 3:4], float(D) ** -0.5))
            for r in range(2):
                act.activation(scol[:, 1 + r:2 + r], cols[:, 1 + r:2 + r], ACT.Copy, scale=scol[:, 0:1]).then_inc(sc_ready, 1)
            act.wait_ge(sc_ready, 2)

            def softplus(c, r):
                n = 2 * c + r
                act.wait_ge(pe_qk, n + 1)
                if c:
                    act.wait_ge(sp_done, n - 1)
                act.activation(ebuf[r][:, :], PS[r][:, :], ACT.Abs, scale=scol[:, 0:1], bias=scol[:, 1 + r:2 + r]).then_inc(sp_abs, 1)
                act.activation(xlin[r][:, :], PS[r][:, :], ACT.Identity, scale=scol[:, 0:1], bias=scol[:, 1 + r:2 + r]).then_inc(sp_lin, 1)
                act.wait_ge(sp_abs, n + 1)
                act.activation(ebuf[r][:, :], ebuf[r][:, :], ACT.Exp, scale=-1.0).then_inc(sp_exp, 1)
                act.wait_ge(sp_exp, n + 1)
                act.activation(lbuf[r][:, :], ebuf[r][:, :], ACT.Ln, bias=1.0).then_inc(sp_ln, 1)

            def v1_copy(t):
                c, i = divmod(t, CT)
                act.wait_ge(pe_v1, c + 1)
                if t == 0:
                    act.wait_ge(z_vb1, 2)
                if t >= 2:
                    act.wait_ge(pe_pv, t - 1)
                for g in range(G):
                    ps = slice(32 * g, 32 * g + 32)
                    ins = act.copy(Vb1[t % 2][ps, :, g, 0:D], PS[2][ps, i * C:(i + 1) * C].rearrange("p (h d) -> p h d", d=D))
                ins.then_inc(v1_ready, 1)

            def norm_start(c):
                a, b = c * CT, (c + 1) * CT
                act.wait_ge(mv_ready, b)
                act.wait_ge(ld_cst, 16)
                link(act.activation(lnv[:, a:b], mv[:, a:b, 1], ACT.Ln, bias=col(K_COEF + 3)))
                act.activation(r0[:, a:b], lnv[:, a:b], ACT.Exp, scale=-0.5).then_inc(r0_ready, 1)

            def apply_norm(c, src, dst):
                act.wait_ge(shift_ready, c + 1)
                for t in range(c * CT, (c + 1) * CT - (CT // 2 if c == 3 * NC - 1 else 0)):
                    act.activation(dst(t), src(t), ACT.Identity, scale=rstd[:, t:t + 1],
                                   bias=shift[:, t % NT:t % NT + 1]).then_inc(normed, 1)

            def x1T_copy(c):
                act.wait_ge(pe_t1, CT * (c + 1))
                dst = x1T[:, :].rearrange("p (s b) -> p b s", b=B)[:, c * 4 * CT:(c + 1) * 4 * CT, :]
                act.copy(dst, PSS[1][:, 1, :].rearrange("p (b s) -> p b s", s=S)).then_inc(x1T_ready, 1)

            softplus(0, 0)
            softplus(0, 1)
            act.wait_ge(pe_bias, 1)
            act.activation(obias[:, :], PS7[:, 0:1], ACT.Identity, bias=cols[:, 3:4]).then_inc(bias_ready, 1)
            act.wait_ge(ld_cst, 16)
            widen_act(act, 0)
            for k in range(NT + 6):
                if k == 0:
                    softplus(1, 0)
                    softplus(1, 1)
                if k < NT:
                    v1_copy(k)
                if k == 1:
                    act.wait_ge(ld_blank, 16)
                    act.wait_ge(z_cos, 1)
                if 1 <= k <= CT:
                    for e in range(2 * k - 2, 2 * k):
                        rows = slice(e * CAP, (e + 1) * CAP)
                        act.dma_start(slots_d[rows, :].rearrange("(p j) n -> p (j n)", j=4), blank_sb[:, :]).then_inc(init_d, 16)
                        act.dma_start(picks_d[rows, :].rearrange("(p j) n -> p (j n)", j=4), zero_sb[:, :]).then_inc(init_d, 16)
                if k % CT == 2 and k // CT + 1 < NC:
                    widen_act(act, k // CT + 1)
                if k % CT == 3 and k // CT + 2 < NC:
                    softplus(k // CT + 2, 0)
                    softplus(k // CT + 2, 1)
                for c in due(k, 7):
                    norm_start(c)
                if k == NT:
                    widen_act(act, NC)
                for c in due(k, 8):
                    if c >= 2:
                        act.wait_ge(pe_t1, CT * (c - 1))
                    apply_norm(c, out_psum, lambda t: x1n[c % 2][:, t % CT, :])
                for c in due(k, 9):
                    x1T_copy(c)
            widen_act(act, NC + 1)

            def v2_copy(t):
                c, i = divmod(t, CT)
                act.wait_ge(pe_v2, c + 1)
                if t == 0:
                    act.wait_ge(z_vb, 2)
                if t >= 2:
                    act.wait_ge(pe_pv, NT + t - 1)
                for g in range(G):
                    for k in range(2):
                        src = 32 * (2 * (g // 2) + k)
                        ins = act.copy(Vb2[t % 2][32 * g:32 * g + 32, k, :, g, 0:D],
                                       PS[2][src:src + 32, i * C:(i + 1) * C].rearrange("p (h d) -> p h d", d=D))
                ins.then_inc(v2_ready, 1)

            def exp2(t):
                act.wait_ge(sub_done, t + 1)
                act.activation(SC[t % 2][:, :, :], SC[t % 2][:, :, :], ACT.Exp).then_inc(exp_done, 1)

            def x2T_copy(c):
                act.wait_ge(pe_t2, c + 1)
                if c:
                    act.wait_ge(pe_gate, c)
                act.copy(x2T[:, :], PS[0][:, :]).then_inc(x2T_ready, 1)

            def gate_exp_step(c):
                act.wait_ge(gate_sub, c + 1)
                act.activation(ge[:, :, :], gl[:, :, :], ACT.Exp).then_inc(gate_exp, 1)

            for k in range(NT + 9):
                if k < NT:
                    exp2(k)
                for c in due(k, 12):
                    gate_exp_step(c)
                for c in due(k, 11):
                    x2T_copy(c)
                for c in due(k, 9):
                    norm_start(NC + c)
                if k > CT and k % CT == 1 and k // CT + 1 < NC:
                    widen_act(act, NC + k // CT + 1)
                if 1 <= k <= NT:
                    v2_copy(k - 1)
                for c in due(k, 9):
                    apply_norm(NC + c, lambda t: out_psum(t)[:, None, :].to_broadcast([128, K2, C]), lambda t: xrow[:, t - NT, :, 0:C])

            def xeT_copy(e):
                act.wait_ge(pe_te, e + 1)
                if e >= 2:
                    act.wait_ge(pe_h, e - 1)
                act.copy(xeT[e % 2][:, :], PS[0][:, :]).then_inc(xeT_ready, 1)

            def silu(e):
                act.wait_ge(pe_h, e + 1)
                if e >= 2:
                    act.wait_ge(hid_ready, e - 1)
                pa, pm = expert_psum(e)[0], expert_psum(e)[2]
                act.activation(sil[e % 2][:, 0, :], pa, ACT.Silu)
                act.activation(sil[e % 2][64:128, 1, :], pm[0:64, :], ACT.Silu).then_inc(sil_ready, 1)

            xeT_copy(0)
            xeT_copy(1)
            silu(0)
            for e in range(E):
                if e + 2 < E:
                    xeT_copy(e + 2)
                if e + 1 < E:
                    silu(e + 1)
                weigh(act, e)
            act.preload_act_table_set("natural_log_exp_and_others")
            for c in range(NC + 1):
                if c < NC:
                    norm_start(2 * NC + c)
                if c:
                    apply_norm(2 * NC + c - 1, lambda t: Z[:, t % NT, :], lambda t: R[:, t % NT, :])

        @block.tensor
        def _(pe):
            def project1(c):
                pe.wait_ge(ld_x[c], 16)
                if c == 0:
                    pe.wait_ge(ld_w1, 16)
                for r in range(2):
                    if c:
                        pe.wait_ge(sp_lin, 2 * c - 1 + r)
                    pe.matmul(PS[r][:, :], w1[:, r, :], xT[:, c * CH:(c + 1) * CH], start=True, stop=True).then_inc(pe_qk, 1)

            def project_v1(c):
                if c:
                    pe.wait_ge(v1_ready, CT * c)
                for i in range(CT):
                    t = c * CT + i
                    ins = pe.matmul(PS[2][:, i * C:(i + 1) * C], xT[:, t * T:(t + 1) * T], w1[:, 2, :], start=True, stop=True)
                ins.then_inc(pe_v1, 1)

            def scores1(t):
                c, i = divmod(t, CT)
                if i == 0:
                    pe.wait_ge(sp_done, 2 * c + 2)
                    pe.wait_ge(widened[c % 2], widened_dma(c))
                    pe.wait_ge(wide_pool, c + 1)
                    pe.wait_ge(wide_act, c + 1)
                if t >= 2:
                    pe.wait_ge(p1_ready, t - 1)
                for j in range(G):
                    a = i * T + j * S
                    ins = pe.matmul(PSS[0][32 * j:32 * j + 32, t % 2, :], kT[c % 2][:, a:a + S], wide[c % 2][:, :, a:a + S],
                                    start=True, stop=True)
                ins.then_inc(pe_s1, 1)

            def values1(t):
                pe.wait_ge(p1_ready, t + 1)
                pe.wait_ge(v1_ready, t + 1)
                if t:
                    pe.wait_ge(o_norm, t)
                else:
                    pe.wait_ge(bias_ready, 1)
                for i in range(I):
                    for g in range(G):
                        h = I * g + i
                        ins = pe.matmul(pv_psum[32 * g:32 * g + 32, i * G * V9:(i + 1) * G * V9],
                                        P1[t % 2][:, h, :], Vb1[t % 2][:, h, :, :].rearrange("p g v -> p (g v)"), start=True, stop=True)
                ins.then_inc(pe_pv, 1)

            issued = {"rope": 0, "out": 0, "turn": 0, "gate": 0, "count": 0}

            def bank0_free():
                if issued["out"]:
                    pe.wait_ge(normed, NT + CT * issued["out"])
                if issued["turn"]:
                    pe.wait_ge(x2T_ready, issued["turn"])

            def bank1_free():
                pe.wait_ge(rope_mul, issued["rope"])
                pe.wait_ge(rope_cos, issued["rope"])
                if issued["gate"]:
                    pe.wait_ge(gate_sub, issued["gate"])
                if issued["count"]:
                    pe.wait_ge(slot_ready, issued["count"])

            def project_out(cc):
                layer, c = divmod(cc, NC)
                pe.wait_ge(o_ready, CT * (cc + 1))
                if cc == 0:
                    pe.wait_ge(xb_ready, 1)
                    pe.wait_ge(ld_cst, 16)
                if layer:
                    bank0_free()
                    issued["out"] += 1
                elif c:
                    pe.wait_ge(normed, CT * c)
                res = x1T if layer else xb
                for t in range(cc * CT, (cc + 1) * CT):
                    i = t - layer * NT
                    pe.matmul(out_psum(t), OT[t % (2 * CT)][:, :], w2[:, 3, :] if layer else w1[:, 3, :], start=True, stop=False)
                    ins = pe.matmul(out_psum(t), res[:, i * T:(i + 1) * T], ident, start=False, stop=True)
                ins.then_inc(pe_out, 1)

            def turn1(c):
                if c:
                    pe.wait_ge(x1T_ready, c)
                for i in range(CT):
                    pe.wait_ge(normed, c * CT + i + 1)
                    pe.transpose(PSS[1][:, 1, i * T:(i + 1) * T], x1n[c % 2][:, i, :], ident).then_inc(pe_t1, 1)

            def rope(n):
                w, c = ROPES[n]
                if n == 0:
                    pe.wait_ge(ld_w2, 16)
                    pe.wait_ge(ld_ctx, 16)
                    pe.wait_ge(sp_lin, 2 * NC)
                else:
                    bank1_free()
                issued["rope"] += 1
                if ROPES[n] == ("q", 0):
                    pe.wait_ge(x1T_ready, NC)
                src = (ctxT if w == "k" else x1T)[:, c * CH:(c + 1) * CH]
                pe.matmul(PS[1][:, :], w2[:, 1 if w == "k" else 0, :], src, start=True, stop=True).then_inc(pe_rope, 1)

            def values2_in(c):
                if c == 0:
                    pe.wait_ge(v1_ready, NT)
                else:
                    pe.wait_ge(v2_ready, CT * c)
                for i in range(CT):
                    t = c * CT + i
                    ins = pe.matmul(PS[2][:, i * C:(i + 1) * C], ctxT[:, t * T:(t + 1) * T], w2[:, 2, :], start=True, stop=True)
                ins.then_inc(pe_v2, 1)

            def scores2(t):
                c, i = divmod(t, CT)
                if t == 0:
                    pe.wait_ge(rows_ready, 2)
                if i == 0:
                    pe.wait_ge(rope_done, ROPES.index(("q", c)) + 1)
                    pe.wait_ge(widened[c % 2], widened_dma(NC + c))
                    pe.wait_ge(wide_pool, NC + c + 1)
                    pe.wait_ge(wide_act, NC + c + 1)
                if t >= 2:
                    pe.wait_ge(sub_done, t - 1)
                if t == 1:
                    pe.wait_ge(o_norm, NT)
                    pe.wait_ge(x1T_ready, NC)
                for half in range(2):
                    for b in range(2):
                        a = t * T + b * B
                        pe.matmul(PSS[t % 2][64 * b:64 * b + 64, half, :], mrow[:, a:a + B],
                                  nrow[:, None, a:a + B].to_broadcast([128, H // 2, B]), start=True, stop=False)
                for half in range(2):
                    for b in range(2):
                        a = i * T + b * B
                        ins = pe.matmul(PSS[t % 2][64 * b:64 * b + 64, half, :], qT2[c % 2][:, a:a + B],
                                        wide[c % 2][:, half * 8:half * 8 + 8, a:a + B], start=False, stop=True)
                ins.then_inc(pe_s2, 1)

            def values2(t):
                pe.wait_ge(pt_ready, t + 1)
                pe.wait_ge(v2_ready, t + 1)
                if t:
                    pe.wait_ge(o_norm, NT + t)
                for i in range(I):
                    for k in range(2):
                        for g in range(G):
                            h = I * g + i
                            ins = pe.matmul(pv_psum[32 * g:32 * g + 32, i * G * V9:(i + 1) * G * V9], PT[t % 2][:, h, k, :],
                                            Vb2[t % 2][:, k, h, :, :].rearrange("p g v -> p (g v)"), start=(k == 0), stop=(k == 1))
                ins.then_inc(pe_pv, 1)

            def turn2(c):
                bank0_free()
                issued["turn"] += 1
                for i in range(CT):
                    t = c * CT + i
                    pe.wait_ge(normed, NT + t + 1)
                    ins = pe.transpose(PS[0][:, i * T:(i + 1) * T], xrow[:, t, 0, 0:C], ident)
                ins.then_inc(pe_t2, 1)

            def gate(c):
                if c == 0:
                    pe.wait_ge(ld_wg, 16)
                bank1_free()
                issued["gate"] += 1
                pe.wait_ge(x2T_ready, c + 1)
                for i in range(CT):
                    ins = pe.matmul(gate_psum[:, i * E:(i + 1) * E], x2T[:, i * T:(i + 1) * T], wg[:, :], start=True, stop=True)
                ins.then_inc(pe_gate, 1)

            def count(c):
                pe.wait_ge(mem_ready, c + 1)
                bank1_free()
                issued["count"] += 1
                if c == 0:
                    pe.wait_ge(ones_ready, 2)
                pe.matmul(cum_psum, tri[:, :], mem[:, :, :].rearrange("p t e -> p (t e)"), start=True, stop=True)
                for j in range(CT):
                    m = CT - j
                    ins = pe.matmul(cum_psum[:, (j + 1) * E:], ones[:, :], mem[:, j:j + 1, :].to_broadcast([128, m, E]),
                                    start=False, stop=True, skip_group_check=True)
                ins.then_inc(pe_cum, 1)

            project1(0)
            pe.wait_ge(ld_cols, 16)
            pe.matmul(PS7[:, 0:1], w1[:, 3, :], cols[:, 4:5], start=True, stop=True).then_inc(pe_bias, 1)
            for k in range(NT + 6):
                if k < NT:
                    scores1(k)
                if k == 0:
                    project1(1)
                if k % CT == 2 and k // CT + 2 < NC:
                    project1(k // CT + 2)
                if 2 <= k <= NT + 1:
                    values1(k - 2)
                for c in due(k, 7):
                    project_out(c)
                if k % CT == 0 and k < NT:
                    project_v1(k // CT)
                if k == NT - 3:
                    rope(0)
                if k == NT:
                    rope(1)
                for c in due(k, 9):
                    turn1(c)
            rope(2)
            for k in range(NT + 11):
                if k < NT:
                    scores2(k)
                if k and k % CT == 0 and k // CT + 1 < NC:
                    rope(2 * (k // CT + 1))
                for c in due(k, 1):
                    values2_in(c)
                if k % CT == 2 and k // CT + 1 < NC:
                    rope(2 * (k // CT + 1) + 1)
                for c in due(k, 8):
                    project_out(NC + c)
                for c in due(k, 11):
                    turn2(c)
                for c in due(k, 12):
                    gate(c)
                for c in routed(k - 1):
                    count(c)
                if 3 <= k <= NT + 2:
                    values2(k - 3)

            def turn_rows(e):
                pe.wait_ge(et_in[e], 16)
                if e:
                    pe.wait_ge(xeT_ready, e)
                for j in range(CT):
                    ins = pe.transpose(PS[0][:, j * T:(j + 1) * T], et[e][:, j, 0:C], ident)
                ins.then_inc(pe_te, 1)

            def hidden(e):
                if e == 0:
                    pe.wait_ge(ld_fc, 16)
                pe.wait_ge(xeT_ready, e + 1)
                if e >= 2:
                    pe.wait_ge(hid_ready, e - 1)
                pa, pg, pm = expert_psum(e)
                x = xeT[e % 2][:, :]
                pe.matmul(pa, fc[:, e, 0:128], x, start=True, stop=True)
                pe.matmul(pg, fc[:, e, 128:256], x, start=True, stop=True)
                pe.matmul(pm[0:64, :], fc[:, e, 256:320], x, start=True, stop=True)
                pe.matmul(pm[64:128, :], fc[:, e, 320:384], x, start=True, stop=True).then_inc(pe_h, 1)

            def expert_out(e):
                if e == 0:
                    pe.wait_ge(ld_pj, 32)
                else:
                    pe.wait_ge(ys_ready, CT * e)
                pe.wait_ge(hid_ready, e + 1)
                for j in range(CT):
                    o = PS7[:, j * C:(j + 1) * C]
                    pe.matmul(o, hid[e % 2][:, 0, j * T:(j + 1) * T], pj0[:, e, :], start=True, stop=False)
                    ins = pe.matmul(o, hid[e % 2][:, 1, j * T:(j + 1) * T], pj1[:, e, :], start=False, stop=True)
                ins.then_inc(pe_y, 1)

            turn_rows(0)
            turn_rows(1)
            hidden(0)
            for e in range(E):
                if e + 2 < E:
                    turn_rows(e + 2)
                if e + 1 < E:
                    hidden(e + 1)
                expert_out(e)

        @block.vector
        def _(dve):
            chain = [0]

            def link(ins):
                chain[0] += 1
                ins.then_inc(dve_chain, 1)
                dve.wait_ge(dve_chain, chain[0])

            for i in range(2):
                link(dve.memset(Vb1[i][:, :, :, :], 0.0))
                for g in range(G):
                    ins = dve.memset(Vb1[i][32 * g:32 * g + 32, :, g, D:V9], 1.0)
                ins.then_inc(z_vb1, 1)
            dve.memset(carry[0][:, :], 0.0)
            dve.memset(mem[:, :, :], 0.0)
            for i in range(2):
                link(dve.memset(Vb2[i][:, :, :, :, :].rearrange("p k h g v -> p (k h g v)"), 0.0))
                for g in range(G):
                    ins = dve.memset(Vb2[i][32 * g:32 * g + 32, :, :, g, D:V9], 1.0)
                ins.then_inc(z_vb, 1)

            def softplus(c, r):
                n = 2 * c + r
                dve.wait_ge(sp_ln, n + 1)
                dve.wait_ge(sp_lin, n + 1)
                link(dve.scalar_tensor_tensor(xlin[r][:, :], xlin[r][:, :], 0.0, lbuf[r][:, :], ALU.max, ALU.add))
                if c >= 2 and r == 0:
                    dve.wait_ge(widened[c % 2], widened_dma(c - 2))
                    dve.wait_ge(wide_pool, c - 1)
                    dve.wait_ge(wide_act, c - 1)
                if c >= 2 and r == 1:
                    dve.wait_ge(pe_s1, CT * (c - 1))
                if c:
                    dve.wait_ge(t_ready, n - 1)
                else:
                    link(dve.tensor_scalar(wbuf[r][:, :], ebuf[r][:, :], 1.0, -1.0, ALU.add, ALU.add))
                    link(dve.tensor_tensor(wbuf[r][:, :], ebuf[r][:, :], wbuf[r][:, :], ALU.subtract))
                dst = (qT if r == 0 else kT)[c % 2]
                dve.tensor_tensor(dst[:, :], xlin[r][:, :], wbuf[r][:, :], ALU.add).then_inc(sp_done, 1)

            def causal(t):
                dve.wait_ge(pe_s1, t + 1)
                if t == 0:
                    dve.wait_ge(ld_cst, 16)
                if t >= 2:
                    dve.wait_ge(pe_pv, t - 1)
                dve.tensor_tensor(P1[t % 2][:, :, :], PSS[0][:, t % 2, :].rearrange("p (h s) -> p h s", s=S),
                                  cst[:, None, K_CAUSAL:K_CAUSAL + S].to_broadcast([128, H, S]), ALU.mult).then_inc(p1_ready, 1)

            pv = pv_psum.rearrange("p (i g v) -> p i g v", i=I, g=G)

            def weight_sums(t):
                dve.wait_ge(pe_pv, t + 1)
                dve.reciprocal(rden[:, t % 2, :, :], pv[:, :, :, D]).then_inc(rden_ready, 1)

            def divide(t):
                dve.wait_ge(rden_ready, t + 1)
                dve.tensor_tensor(O[t % 2][:, :, :, :].rearrange("p g i d -> p i g d"), pv[:, :, :, 0:D],
                                  rden[:, t % 2, :, :, None].to_broadcast([128, I, G, D]), ALU.mult).then_inc(o_norm, 1)

            def turn_out(t):
                dve.wait_ge(o_norm, t + 1)
                if t >= 2 * CT:
                    dve.wait_ge(pe_out, t // CT - 1)
                dve.transpose(OT[t % (2 * CT)][:, :], O[t % 2][:, :, :, :].rearrange("p g i d -> p (g i d)")).then_inc(o_ready, 1)

            def moments(c, src):
                for t in range(c * CT, (c + 1) * CT):
                    ins = dve.bn_stats(stats[:, t, :], src(t))
                link(ins)
                for t in range(c * CT, (c + 1) * CT):
                    dve.bn_aggr(mv[:, t, :], stats[:, t, :]).then_inc(mv_ready, 1)

            def moments_out(c):
                dve.wait_ge(pe_out, c + 1)
                moments(c, out_psum)

            def newton(c):
                a, b = c * CT, (c + 1) * CT
                dve.wait_ge(r0_ready, c + 1)
                link(dve.tensor_tensor(r1[:, a:b], r0[:, a:b], r0[:, a:b], ALU.mult))
                link(dve.scalar_tensor_tensor(r1[:, a:b], mv[:, a:b, 1], EPS, r1[:, a:b], ALU.add, ALU.mult))
                link(dve.tensor_scalar(r1[:, a:b], r1[:, a:b], -0.5, 1.5, ALU.mult, ALU.add))
                link(dve.tensor_tensor(rstd[:, a:b], r1[:, a:b], r0[:, a:b], ALU.mult))

            def newton_shift(c):
                newton(c)
                a, b = c * CT, (c + 1) * CT
                dve.scalar_tensor_tensor(shift[:, a % NT:a % NT + CT], mv[:, a:b, 0], -1.0, rstd[:, a:b],
                                         ALU.mult, ALU.mult).then_inc(shift_ready, 1)

            softplus(0, 0)
            softplus(0, 1)
            for k in range(NT + 5):
                if 3 <= k <= NT + 2:
                    weight_sums(k - 3)
                    divide(k - 3)
                    turn_out(k - 3)
                if k < NT:
                    causal(k)
                if k % CT == 1 and k // CT + 1 < NC:
                    softplus(k // CT + 1, 0)
                if k % CT == 2 and k // CT + 1 < NC:
                    softplus(k // CT + 1, 1)
                for c in due(k, 7):
                    moments_out(c)
                if k == 2:
                    dve.memset(ones[:, :], 1.0).then_inc(ones_ready, 1)
                    dve.tensor_copy(tri[:, :], cst[:, K_TRI:K_TRI + 128]).then_inc(ones_ready, 1)
                for c in due(k, 8):
                    newton_shift(c)
                if k == NT - 2:
                    rope_products(dve, 0)
                if k == NT + 2:
                    rope_products(dve, 1)

            def scores_of(t):
                return PSS[t % 2][:, :, :].rearrange("p a (h b) -> p (a h) b", b=B)

            def maxima(t):
                dve.wait_ge(pe_s2, t + 1)
                dve.tensor_reduce(mx2[:, t % 2, :], scores_of(t), AX.X, ALU.max).then_inc(max_ready, 1)

            def subtract(t):
                dve.wait_ge(max_ready, t + 1)
                if t >= 2:
                    dve.wait_ge(pt_ready, t - 1)
                dve.tensor_tensor(SC[t % 2][:, :, :], scores_of(t), mx2[:, t % 2, :, None].to_broadcast([128, H, B]),
                                  ALU.subtract).then_inc(sub_done, 1)

            def turn_probs(t):
                dve.wait_ge(exp_done, t + 1)
                if t >= 2:
                    dve.wait_ge(pe_pv, NT + t - 1)
                dve.transpose(PT[t % 2][:, :, :, :].rearrange("p h k s -> p (h k s)"), SC[t % 2][:, :, :].rearrange("p h b -> p (h b)")).then_inc(pt_ready, 1)

            def route_a(c):
                dve.wait_ge(pe_gate, c + 1)
                p = gate_psum.rearrange("p (t e) -> p t e", e=E)
                link(dve.tensor_reduce(g1[:, :], p, AX.X, ALU.max))
                dve.tensor_tensor(gl[:, :, :], p, g1[:, :, None].to_broadcast([128, CT, E]), ALU.subtract).then_inc(gate_sub, 1)

            def route_b(c):
                dve.wait_ge(gate_exp, c + 1)
                link(dve.tensor_reduce(g1[:, :], ge[:, :, :], AX.X, ALU.add))
                link(dve.reciprocal(g1[:, :], g1[:, :]))
                link(dve.tensor_tensor(gs[:, :, :], ge[:, :, :], g1[:, :, None].to_broadcast([128, CT, E]), ALU.mult))
                rank = cst[:, None, K_RANK:K_RANK + E].to_broadcast([128, CT, E])
                for k in range(K2):
                    link(dve.tensor_reduce(gm[:, k, :], gs[:, :, :], AX.X, ALU.max))
                    link(dve.tensor_tensor(gt[:, :, :], gs[:, :, :], gm[:, k, :, None].to_broadcast([128, CT, E]), ALU.is_equal))
                    link(dve.tensor_tensor(gt[:, :, :], gt[:, :, :], rank, ALU.mult))
                    link(dve.tensor_reduce(g1[:, :], gt[:, :, :], AX.X, ALU.max))
                    link(dve.tensor_tensor(pick[:, k, :, :], rank, g1[:, :, None].to_broadcast([128, CT, E]), ALU.is_equal))
                    if k == 0:
                        link(dve.scalar_tensor_tensor(gs[:, :, :], pick[:, 0, :, :], -2.0, gs[:, :, :], ALU.mult, ALU.add))
                if c:
                    dve.wait_ge(pe_cum, c)
                dve.tensor_tensor(mem[:, 0:CT, :], pick[:, 0, :, :], pick[:, 1, :, :], ALU.add).then_inc(mem_ready, 1)
                dve.tensor_copy(xrow[:, c * CT:(c + 1) * CT, :, C + 1].rearrange("p t k -> p k t"), gm[:, :, :])

            def route_c(c):
                dve.wait_ge(pe_cum, c + 1)
                cum = cum_psum.rearrange("p (t e) -> p t e", e=E)
                base = cst[:, None, K_BASE:K_BASE + E].to_broadcast([128, CT, E])
                link(dve.tensor_tensor(pos[:, :, :], cum[:, 0:CT, :], carry[c % 2][:, None, :].to_broadcast([128, CT, E]), ALU.add))
                link(dve.tensor_scalar(over[:, :, :], pos[:, :, :], float(CAP), UNUSED, ALU.is_ge, ALU.mult))
                dve.tensor_tensor(carry[(c + 1) % 2][:, :], cum[:, CT, :], carry[c % 2][:, :], ALU.add)
                link(dve.tensor_tensor(pos[:, :, :], pos[:, :, :], base, ALU.add))
                link(dve.tensor_tensor(pos[:, :, :], pos[:, :, :], over[:, :, :], ALU.add))
                link(dve.tensor_tensor(pp[:, :, :, :], pos[:, None, :, :].to_broadcast([128, K2, CT, E]), pick[:, :, :, :], ALU.mult))
                link(dve.tensor_reduce(psel[:, :, :], pp[:, :, :, :], AX.X, ALU.add))
                dve.tensor_copy(slot[:, c * CT:(c + 1) * CT, :].rearrange("p t k -> p k t"), psel[:, :, :]).then_inc(slot_ready, 1)

            rope_products(dve, 2)
            dve.wait_ge(ld_dest, 16)
            dve.tensor_copy(xrow[:, :, :, C].bitcast(U32), dest[:, :, :])
            for k in range(NT + 11):
                if 4 <= k <= NT + 3:
                    weight_sums(NT + k - 4)
                for c in due(k, 9):
                    moments_out(NC + c)
                if 2 <= k <= NT + 1:
                    turn_probs(k - 2)
                if 4 <= k <= NT + 3:
                    divide(NT + k - 4)
                if k < NT:
                    maxima(k)
                if 4 <= k <= NT + 3:
                    turn_out(NT + k - 4)
                if k < NT:
                    subtract(k)
                for c in due(k, 9):
                    newton_shift(NC + c)
                if k and k % CT == 0 and k // CT + 1 < NC:
                    rope_products(dve, 2 * (k // CT + 1))
                if k % CT == 2 and k // CT + 1 < NC:
                    rope_products(dve, 2 * (k // CT + 1) + 1)
                for c in routed(k - 1):
                    route_c(c)
                for c in due(k, 12):
                    route_a(c)
                for c in routed(k):
                    route_b(c)

            dve.wait_ge(pe_pv, 2 * NT)
            for i in range(2):
                link(dve.memset(hid[i][0:64, 1, :], 0.0))
            for e in range(E):
                pa, pg, pm = expert_psum(e)
                dve.wait_ge(sil_ready, e + 1)
                if e >= 2:
                    dve.wait_ge(pe_y, e - 1)
                dve.tensor_tensor(hid[e % 2][:, 0, :], sil[e % 2][:, 0, :], pg, ALU.mult)
                dve.tensor_tensor(hid[e % 2][64:128, 1, :], sil[e % 2][64:128, 1, :], pm[64:128, :], ALU.mult).then_inc(hid_ready, 1)

            for c in range(NC + 1):
                if c < NC:
                    dve.wait_ge(y_sum, c + 1)
                    a, b = c * CT, (c + 1) * CT
                    link(dve.tensor_tensor(Z[:, a:b, :], Z[:, a:b, :], xrow[:, a:b, 0, 0:C], ALU.add))
                    moments(2 * NC + c, lambda t: Z[:, t - 2 * NT, :])
                if c:
                    newton_shift(2 * NC + c - 1)
            dve.wait_ge(shift_ready, 3 * NC)
            for t in range(NT - CT // 2, NT):
                dve.tensor_scalar(R[:, t, :], Z[:, t, :], mv[:, 2 * NT + t, 0:1], rstd[:, 2 * NT + t:2 * NT + t + 1],
                                  ALU.subtract, ALU.mult).then_inc(last_half, 1)


def _lay_out(i):
    f = lambda n: np.asarray(i[n])
    wq, wkv = f("L0_xattn_W_q"), f("L0_xattn_W_kv")
    wk, wv = wkv[:, :C], wkv[:, C:]
    fc = f("L0_ffn_c_fc")
    fc = np.concatenate([fc[:, :, 0:128], fc[:, :, F:F + 128], fc[:, :, 128:F], fc[:, :, F + 128:]], axis=2)
    k, dest, blank = constants()
    return {
        "xT": np.ascontiguousarray(f("x").transpose(2, 1, 0).reshape(C, N)),
        "ctxT": np.ascontiguousarray(f("ctx_1024").transpose(2, 0, 1).reshape(C, N)),
        "mask": np.ascontiguousarray(f("mask_BxS2_bf1").reshape(1, N)).view(np.uint8),
        "cols": np.stack([np.repeat(f("L0_attn_beta"), D), f("L0_attn_bq"), f("L0_attn_bk"), f("L0_attn_bo"), f("L0_attn_bv")],
                         axis=1),
        "w1": np.concatenate([f(n).T for n in ("L0_attn_Wq", "L0_attn_Wk", "L0_attn_Wv", "L0_attn_Wo")], axis=1),
        "w2": np.concatenate([wq, wk, wv, f("L0_xattn_W_c")], axis=1),
        "wg": f("L0_ffn_w_gate"),
        "fc": np.ascontiguousarray(fc.transpose(1, 0, 2).reshape(C, E * 2 * F)),
        "proj": f("L0_ffn_c_proj"),
        "consts": k, "dest": dest, "blank": blank,
    }


def kernel(**inputs):
    import concourse.bacc as bacc
    from concourse.bass_utils import run_bass_kernel_spmd

    nc = bacc.Bacc("TRN2", target_bir_lowering=False, num_devices=1)
    arrays, args = {}, []
    for name, a in _lay_out(inputs).items():
        a = np.ascontiguousarray(a)
        arrays[f"in_{name}"] = a
        args.append(nc.dram_tensor(f"in_{name}", a.shape, mybir.dt.from_np(a.dtype), kind="ExternalInput").ap())
    out = nc.dram_tensor("out_0", (S, B, C), F32, kind="ExternalOutput").ap()
    decoder_layer(nc, *args, out)
    r = run_bass_kernel_spmd(nc, [arrays], core_ids=[0])
    return r.results[0]["out_0"]
```
